# Optimizing a Trainium2 kernel written in Bass

```python
import numpy as np
import jax
import jax.numpy as jnp

def _softmax(x, axis=-1):
    return jax.nn.softmax(x, axis=axis)

def _gelu(x):
    return jax.nn.gelu(x, approximate=True)

def _silu(x):
    return jax.nn.silu(x)

def _sigmoid(x):
    return jax.nn.sigmoid(x)

def _layernorm(x, axis=-1, eps=1e-05):
    m = jnp.mean(x, axis=axis, keepdims=True)
    v = jnp.var(x, axis=axis, keepdims=True)
    return (x - m) / jnp.sqrt(v + eps)

def _scatter_add(tgt, idx, src, axis=0):
    return tgt.at[idx].add(src)

def _segment_sum(src, seg, n):
    return jax.ops.segment_sum(src, seg, n)
kernel_name = 'mk_gnn_resnorm_d4_gnn_r8_4eef00'

def setup_inputs(seed: int=0):
    np.random.seed(seed)
    _w = jnp.asarray

    def _rec_inputs():
        import jax
        import jax.numpy as jnp
        _gk = jax.random.key(seed)
        x = -0.0005121 + 1.001 * jax.random.normal(jax.random.fold_in(_gk, 1), (6250, 64), jnp.float32)
        _s = jax.random.randint(jax.random.fold_in(_gk, 2), (100000,), 0, 6250, jnp.int32)
        _d = jax.random.randint(jax.random.fold_in(_gk, 3), (100000,), 0, 6250, jnp.int32)
        _loop = jnp.arange(6250, dtype=jnp.int32)
        src = jnp.concatenate([_s, _d, _loop])
        dst = jnp.concatenate([_d, _s, _loop])
        _o = jnp.argsort(dst, stable=True)
        src = src[_o]
        dst = dst[_o]
        edge_attr_16 = 0.000196303 + 1.00016 * jax.random.normal(jax.random.fold_in(_gk, 12), (206250, 16), jnp.float32)
        edge_attr_64 = -9.77346e-05 + 0.999888 * jax.random.normal(jax.random.fold_in(_gk, 13), (206250, 64), jnp.float32)
        edge_weight = jax.random.uniform(jax.random.fold_in(_gk, 15), (206250,), jnp.float32, 0.0, 1)
        edge_weight_n2 = jax.random.uniform(jax.random.fold_in(_gk, 16), (206250,), jnp.float32, 0.0, 1)
        return (x, src, dst, edge_attr_16, edge_attr_64, edge_weight, edge_weight_n2)
    x, src, dst, edge_attr_16, edge_attr_64, edge_weight, edge_weight_n2 = _rec_inputs()

    def _L0_gnn_setup():
        import jax, jax.numpy as jnp
        import numpy as np
        N = 6250
        E = 100000
        D = 64
        H = 64
        KI = 32
        KM = 32
        DMAX = 1.0

        def _normalize_edges(edges, segment_ids, num_segments):
            s = jax.ops.segment_sum(edges, segment_ids, num_segments=num_segments, indices_are_sorted=True)
            return edges / (s[segment_ids] + 1e-05)
        key = jax.random.key(seed)
        ks = jax.random.split(key, 10)
        nodes = jax.random.normal(ks[0], (N, D), jnp.float32)
        distance = jax.random.uniform(ks[1], (E,), jnp.float32) * DMAX
        receivers = jnp.sort(jax.random.randint(ks[2], (E,), 0, N)).astype(jnp.int32)
        senders = jax.random.randint(ks[3], (E,), 0, N).astype(jnp.int32)
        edges_padding = jnp.ones((E,), jnp.float32)
        mlp_w1 = jax.random.normal(ks[4], (1, H), jnp.float32) * 0.5
        mlp_b1 = jax.random.normal(ks[5], (H,), jnp.float32) * 0.1
        mlp_w2 = jax.random.normal(ks[6], (H, KM), jnp.float32) * 0.2
        mlp_b2 = jax.random.normal(ks[7], (KM,), jnp.float32) * 0.1
        pd_a = jnp.full((1,), 0.5, jnp.float32)
        pd_b = jnp.full((1,), 2.0, jnp.float32)
        gamma_self_w = jax.random.normal(ks[8], (D, KI + KM), jnp.float32) * 0.1
        gamma_gathered_w = jax.random.normal(ks[9], (D, KI + KM), jnp.float32) * 0.1
        gamma_gathered_b = jnp.zeros((KI + KM,), jnp.float32)
        return dict(nodes=nodes, distance=distance, edges_padding=edges_padding, mlp_w1=mlp_w1, mlp_b1=mlp_b1, mlp_w2=mlp_w2, mlp_b2=mlp_b2, pd_a=pd_a, pd_b=pd_b, gamma_self_w=gamma_self_w, gamma_gathered_w=gamma_gathered_w, gamma_gathered_b=gamma_gathered_b, receivers=receivers, senders=senders)
    _L0_gnn_all = _L0_gnn_setup()
    _L0_gnn_in = {k: v for k, v in _L0_gnn_all.items() if k in ('mlp_w1', 'mlp_b1', 'mlp_w2', 'mlp_b2', 'pd_a', 'pd_b', 'gamma_self_w', 'gamma_gathered_w', 'gamma_gathered_b')}
    del _L0_gnn_all

    def _L1_gnn_setup():
        import jax, jax.numpy as jnp
        import numpy as np
        N, E, IN, OUT, ED = (12500, 200000, 64, 64, 16)
        NEG = -1000000000.0
        key = jax.random.key(seed)
        ks = jax.random.split(key, 8)
        x = jax.random.normal(ks[0], (N, IN), jnp.float32)
        edge_index = jax.random.randint(ks[1], (2, E), 0, N, dtype=jnp.int32)
        edge_attr = jax.random.normal(ks[2], (E, ED), jnp.float32)
        Wn = jax.random.normal(ks[3], (IN, OUT), jnp.float32) * (1.0 / np.sqrt(IN))
        We = jax.random.normal(ks[4], (ED, OUT), jnp.float32) * (1.0 / np.sqrt(ED))
        att_src = jax.random.normal(ks[5], (OUT,), jnp.float32) * 0.02
        att_dst = jax.random.normal(ks[6], (OUT,), jnp.float32) * 0.02
        att_edge = jax.random.normal(ks[7], (OUT,), jnp.float32) * 0.02
        return {'x': x, 'edge_index': edge_index, 'edge_attr': edge_attr, 'Wn': Wn, 'We': We, 'att_src': att_src, 'att_dst': att_dst, 'att_edge': att_edge}
    _L1_gnn_all = _L1_gnn_setup()
    _L1_gnn_in = {k: v for k, v in _L1_gnn_all.items() if k in ('Wn', 'We', 'att_src', 'att_dst', 'att_edge')}
    del _L1_gnn_all

    def _L2_gnn_setup():
        import jax, jax.numpy as jnp
        import numpy as np
        N_NODES = 6250
        N_EDGES = 100000
        D_FEAT = 64
        NUM_LAYERS = 3
        EPS = 1e-16

        def _edge_softmax(edge_weight, dst, num_nodes):
            m = jax.ops.segment_max(edge_weight, dst, num_segments=num_nodes)
            e = jnp.exp(edge_weight - m[dst])
            s = jax.ops.segment_sum(e, dst, num_segments=num_nodes)
            return e / (s[dst] + EPS)
        key = jax.random.key(seed)
        k1, k2, k3, k4 = jax.random.split(key, 4)
        x = jax.random.normal(k1, (N_NODES, D_FEAT), dtype=jnp.float32)
        src = jax.random.randint(k2, (N_EDGES,), 0, N_NODES, dtype=jnp.int32)
        dst = jax.random.randint(k3, (N_EDGES,), 0, N_NODES, dtype=jnp.int32)
        edge_index = jnp.stack([src, dst], axis=0)
        edge_weight = jax.random.uniform(k4, (N_EDGES,), dtype=jnp.float32)
        return {'x': x, 'edge_index': edge_index, 'edge_weight': edge_weight}
    _L2_gnn_all = _L2_gnn_setup()
    _L2_gnn_in = {k: v for k, v in _L2_gnn_all.items() if k in ()}
    del _L2_gnn_all

    def _L3_gnn_setup():
        import jax, jax.numpy as jnp
        import numpy as np
        N, E, DN, DE, H = (6250, 100000, 64, 64, 128)
        key = jax.random.key(seed)
        ks = jax.random.split(key, 12)
        s = 0.05
        return {'h': jax.random.normal(ks[0], (N, DN), jnp.float32), 'eh': jax.random.normal(ks[1], (E, DE), jnp.float32), 'W_node1': jax.random.normal(ks[2], (DN, H), jnp.float32) * s, 'b_node1': jax.random.normal(ks[3], (H,), jnp.float32) * s, 'W_node2': jax.random.normal(ks[4], (H, H), jnp.float32) * s, 'W_edge1': jax.random.normal(ks[5], (DE, H), jnp.float32) * s, 'b_edge1': jax.random.normal(ks[6], (H,), jnp.float32) * s, 'W_edge2': jax.random.normal(ks[7], (H, H), jnp.float32) * s, 'W_comb': jax.random.normal(ks[8], (H, DN), jnp.float32) * s, 'W_ue': jax.random.normal(ks[9], (DN, DE), jnp.float32) * s, 'src': jax.random.randint(ks[10], (E,), 0, N, jnp.int32), 'dst': jax.random.randint(ks[11], (E,), 0, N, jnp.int32)}
    _L3_gnn_all = _L3_gnn_setup()
    _L3_gnn_in = {k: v for k, v in _L3_gnn_all.items() if k in ('W_node1', 'b_node1', 'W_node2', 'W_edge1', 'b_edge1', 'W_edge2', 'W_comb', 'W_ue')}
    del _L3_gnn_all
    return {'x': x, 'src': src, 'dst': dst, 'edge_attr_16': edge_attr_16, 'edge_attr_64': edge_attr_64, 'edge_weight': edge_weight, 'edge_weight_n2': edge_weight_n2, 'L0_gnn_mlp_w1': _L0_gnn_in['mlp_w1'], 'L0_gnn_mlp_b1': _L0_gnn_in['mlp_b1'], 'L0_gnn_mlp_w2': _L0_gnn_in['mlp_w2'], 'L0_gnn_mlp_b2': _L0_gnn_in['mlp_b2'], 'L0_gnn_pd_a': _L0_gnn_in['pd_a'], 'L0_gnn_pd_b': _L0_gnn_in['pd_b'], 'L0_gnn_gamma_self_w': _L0_gnn_in['gamma_self_w'], 'L0_gnn_gamma_gathered_w': _L0_gnn_in['gamma_gathered_w'], 'L0_gnn_gamma_gathered_b': _L0_gnn_in['gamma_gathered_b'], 'L1_gnn_Wn': _L1_gnn_in['Wn'], 'L1_gnn_We': _L1_gnn_in['We'], 'L1_gnn_att_src': _L1_gnn_in['att_src'], 'L1_gnn_att_dst': _L1_gnn_in['att_dst'], 'L1_gnn_att_edge': _L1_gnn_in['att_edge'], 'L3_gnn_W_node1': _L3_gnn_in['W_node1'], 'L3_gnn_b_node1': _L3_gnn_in['b_node1'], 'L3_gnn_W_node2': _L3_gnn_in['W_node2'], 'L3_gnn_W_edge1': _L3_gnn_in['W_edge1'], 'L3_gnn_b_edge1': _L3_gnn_in['b_edge1'], 'L3_gnn_W_edge2': _L3_gnn_in['W_edge2'], 'L3_gnn_W_comb': _L3_gnn_in['W_comb'], 'L3_gnn_W_ue': _L3_gnn_in['W_ue']}

def reference(x, src, dst, edge_attr_16, edge_attr_64, edge_weight, edge_weight_n2, L0_gnn_mlp_w1, L0_gnn_mlp_b1, L0_gnn_mlp_w2, L0_gnn_mlp_b2, L0_gnn_pd_a, L0_gnn_pd_b, L0_gnn_gamma_self_w, L0_gnn_gamma_gathered_w, L0_gnn_gamma_gathered_b, L1_gnn_Wn, L1_gnn_We, L1_gnn_att_src, L1_gnn_att_dst, L1_gnn_att_edge, L3_gnn_W_node1, L3_gnn_b_node1, L3_gnn_W_node2, L3_gnn_W_edge1, L3_gnn_b_edge1, L3_gnn_W_edge2, L3_gnn_W_comb, L3_gnn_W_ue):
    import jax
    import jax.numpy as jnp

    def _L0_gnn_ref(nodes, distance, edges_padding, mlp_w1, mlp_b1, mlp_w2, mlp_b2, pd_a, pd_b, gamma_self_w, gamma_gathered_w, gamma_gathered_b, receivers, senders):
        import jax, jax.numpy as jnp
        import numpy as np
        N = 6250
        E = 100000
        D = 64
        H = 64
        KI = 32
        KM = 32
        DMAX = 1.0

        def _normalize_edges(edges, segment_ids, num_segments):
            s = jax.ops.segment_sum(edges, segment_ids, num_segments=num_segments, indices_are_sorted=True)
            return edges / (s[segment_ids] + 1e-05)
        n = nodes.shape[0]
        d = distance.reshape(-1, 1)
        bins = jnp.linspace(0.0, DMAX, KI + 1)
        indicator = jnp.heaviside((bins[None, :-1] - d) * (d - bins[None, 1:]), 0.0)
        h = jax.nn.relu(d @ mlp_w1 + mlp_b1)
        mlp = jax.nn.relu(h @ mlp_w2 + mlp_b2)
        iw = _normalize_edges(indicator, receivers, n)
        mw = _normalize_edges(mlp, receivers, n)
        weights = jnp.hstack((iw, mw)) * edges_padding.reshape(-1, 1)
        a = jnp.clip(pd_a, 0.0, 1.0)
        b = jnp.abs(pd_b)
        edge_pds = jnp.power(jnp.abs(a * nodes[receivers] - (1.0 - a) * nodes[senders]), b)
        gathered = jax.ops.segment_sum(weights * edge_pds, receivers, num_segments=n, indices_are_sorted=True)
        out = nodes @ gamma_self_w + gathered @ gamma_gathered_w + gamma_gathered_b
        return jax.nn.relu(out)

    def _L1_gnn_ref(x, edge_index, edge_attr, Wn, We, att_src, att_dst, att_edge):
        import jax, jax.numpy as jnp
        import numpy as np
        N, E, IN, OUT, ED = (12500, 200000, 64, 64, 16)
        NEG = -1000000000.0
        src, dst = (edge_index[0], edge_index[1])
        n = x.shape[0]
        z = x @ Wn
        e = edge_attr @ We
        s_src = (z @ att_src)[src]
        s_dst = (z @ att_dst)[dst]
        s_edge = e @ att_edge
        score = jax.nn.leaky_relu(s_src + s_dst + s_edge, negative_slope=0.2)
        max_per = jnp.maximum(jax.ops.segment_max(score, dst, num_segments=n), NEG)
        score_exp = jnp.exp(score - max_per[dst])
        denom = jax.ops.segment_sum(score_exp, dst, num_segments=n)
        alpha = score_exp / (denom[dst] + 1e-08)
        msg = (z[src] + e) * alpha[:, None]
        out = jax.ops.segment_sum(msg, dst, num_segments=n)
        return out + x

    def _L2_gnn_ref(x, edge_index, edge_weight):
        import jax, jax.numpy as jnp
        import numpy as np
        N_NODES = 6250
        N_EDGES = 100000
        D_FEAT = 64
        NUM_LAYERS = 3
        EPS = 1e-16

        def _edge_softmax(edge_weight, dst, num_nodes):
            m = jax.ops.segment_max(edge_weight, dst, num_segments=num_nodes)
            e = jnp.exp(edge_weight - m[dst])
            s = jax.ops.segment_sum(e, dst, num_segments=num_nodes)
            return e / (s[dst] + EPS)
        n = x.shape[0]
        src, dst = (edge_index[0], edge_index[1])
        w = _edge_softmax(edge_weight, dst, n)
        final_x = x
        for _ in range(NUM_LAYERS):
            msg = w[:, None] * x[src]
            x = jax.ops.segment_sum(msg, dst, num_segments=n)
            final_x = final_x + x
        final_x = final_x / (NUM_LAYERS + 1)
        return x

    def _L3_gnn_ref(h, eh, W_node1, b_node1, W_node2, W_edge1, b_edge1, W_edge2, W_comb, W_ue, src, dst):
        import jax, jax.numpy as jnp
        import numpy as np
        N, E, DN, DE, H = (6250, 100000, 64, 64, 128)
        hs = h[src]
        hd = h[dst]
        eh_new = 0.8 * eh + 0.2 * (hs * hd @ W_ue)
        m1 = jax.nn.relu(hs @ W_node1 + b_node1) @ W_node2
        m2 = jax.nn.relu(eh_new @ W_edge1 + b_edge1) @ W_edge2
        m = jnp.tanh(m1 * m2 @ W_comb)
        agg = jax.ops.segment_sum(m, dst, num_segments=h.shape[0])
        return agg + h
    edge_index = jnp.stack([src, dst])
    x = _layernorm(x + _L0_gnn_ref(x, edge_weight, edge_weight_n2, L0_gnn_mlp_w1, L0_gnn_mlp_b1, L0_gnn_mlp_w2, L0_gnn_mlp_b2, L0_gnn_pd_a, L0_gnn_pd_b, L0_gnn_gamma_self_w, L0_gnn_gamma_gathered_w, L0_gnn_gamma_gathered_b, dst, src), axis=-1)
    x = _layernorm(x + _L1_gnn_ref(x, edge_index, edge_attr_16, L1_gnn_Wn, L1_gnn_We, L1_gnn_att_src, L1_gnn_att_dst, L1_gnn_att_edge), axis=-1)
    x = _layernorm(x + _L2_gnn_ref(x, edge_index, edge_weight), axis=-1)
    x = _layernorm(x + _L3_gnn_ref(x, edge_attr_64, L3_gnn_W_node1, L3_gnn_b_node1, L3_gnn_W_node2, L3_gnn_W_edge1, L3_gnn_b_edge1, L3_gnn_W_edge2, L3_gnn_W_comb, L3_gnn_W_ue, src, dst), axis=-1)
    return x

_drawn_inputs = setup_inputs


def setup_inputs(seed=0):
    import zlib

    import numpy as np

    out = dict(_drawn_inputs(seed))
    spreads = {'L0_gnn_gamma_gathered_b': (0.0, 0.1)}
    factors = {'L1_gnn_att_dst': 5.925,
     'L3_gnn_b_node1': 4.805,
     'L3_gnn_b_edge1': 3.283,
     'L3_gnn_W_ue': 8.0}
    for name, (base, spread) in spreads.items():
        noise = np.random.default_rng([zlib.crc32(name.encode()), seed]).standard_normal(out[name].shape)
        drawn = base * np.exp(spread * noise) if base else spread * noise
        out[name] = jnp.asarray(drawn.astype(out[name].dtype))
    for name, factor in factors.items():
        out[name] = (out[name] * factor).astype(out[name].dtype)
    return out
```

```python
import numpy as np
from contextlib import ExitStack
import concourse.bass as bass
from concourse import mybir

P = 128
N = 6250
E = 206250
D = 64
H = 128
ED = 16
ROUNDS = 3
BINS = 32
BLOCKS = -(-N // P)
NPAD = BLOCKS * P
TILES = -(-E // P)
UNIT = 4
UNITS = 8
LEAD = 4
ITER = UNIT * UNITS
STEPS = -(-(TILES + BLOCKS - 1) // P) * P
CHUNKS = STEPS // P
TRIPS = STEPS // ITER
PAD_NODE = NPAD - 1
CREDIT = UNITS
FAR = -1.5e38
TINY = 2.0 ** -63
QF = 6
QW = QF * P + 2
L1W = D + 2 + ED
GROUP = 7
assert TRIPS * ITER == STEPS and BLOCKS % GROUP == 0 and PAD_NODE >= N

fp32 = mybir.dt.float32
i32 = mybir.dt.int32
ALU = mybir.AluOpType
ACT = mybir.ActivationFunctionType
AX = mybir.AxisListType


class Program:
    pass


class Chain:

    def __init__(self, eng, sem, start=0):
        self.eng, self.sem, self.n = eng, sem, start

    def __call__(self, ins):
        self.n = self.n + 1
        ins.then_inc(self.sem, 1)
        self.eng.wait_ge(self.sem, self.n)


def done(unit, back=0):
    return unit + (CREDIT + 1 - back)


def bc_last(ap, n):
    return ap.unsqueeze(2).to_broadcast([ap.shape[0], ap.shape[1], n])


def bc_mid(ap, n):
    return ap.unsqueeze(1).to_broadcast([ap.shape[0], n, ap.shape[1]])


def load_edges(nc, m):
    with ExitStack() as ctx:
        sb = lambda name, shape, dt: ctx.enter_context(nc.sbuf_tensor(name, shape, dt))
        cur = sb("dst_cur", [P, CHUNKS, P], i32)
        prev = sb("dst_prev", [P, CHUNKS, P], i32)
        nxt = sb("dst_next", [P, CHUNKS, P], i32)
        srci = sb("src_rows", [P, CHUNKS, P], i32)
        q = sb("edge_fields", [P, CHUNKS, QW], fp32)
        first = sb("first_block", [P, CHUNKS], i32)
        last = sb("last_block", [P, CHUNKS], i32)
        lastf = sb("last_block_f", [P, CHUNKS], fp32)
        extra = sb("extra_steps", [P, CHUNKS], fp32)
        extraT = sb("extra_steps_rows", [CHUNKS, P], fp32)
        extra_row = sb("extra_row", [1, STEPS], fp32)
        run = sb("extra_run", [1, STEPS], fp32)
        ones = sb("ones_row", [1, STEPS], fp32)
        pos = sb("pos_row", [1, STEPS], fp32)
        ps = m.ps[0][0]
        s_in, s_w, s_c, s_row, s_v, s_pos, s_posq, s_q, s_t, s_ct = (
            m.sem(n) for n in ("le_dst", "le_weights", "le_const", "le_row", "le_vec",
                                            "le_pos_out", "le_pos_in", "le_table", "le_pe", "le_rows"))
        flat = lambda off: m.dst_flat[off:off + STEPS * P].rearrange("(c p e) -> p c e", p=P, e=P)
        block = ctx.enter_context(nc.Block())

        @block.vector
        def _(v):
            link = Chain(v, s_v)
            v.wait_ge(s_in, 64)
            link(nc.vector.tensor_scalar(first[:, :], cur[:, :, 0], 7, None, ALU.arith_shift_right))
            link(nc.vector.tensor_scalar(last[:, :], cur[:, :, P - 1], 7, None, ALU.arith_shift_right))
            link(nc.vector.tensor_copy(q[:, :, QF * P + 1], first[:, :]))
            link(nc.vector.tensor_copy(lastf[:, :], last[:, :]))
            link(nc.vector.tensor_tensor(extra[:, :], lastf[:, :], q[:, :, QF * P + 1], ALU.subtract))
            v.wait_ge(s_t, 1)
            nc.vector.tensor_copy(extraT[:, :], ps[0:CHUNKS, 0:P]).then_inc(s_ct, 1)
            link(nc.vector.tensor_copy(q[:, :, 0:P], cur[:, :, :]))
            link(nc.vector.tensor_copy(q[:, :, P:2 * P], srci[:, :, :]))
            link(nc.vector.tensor_tensor(q[:, :, 4 * P:5 * P], cur[:, :, :], prev[:, :, :], ALU.not_equal))
            link(nc.vector.tensor_tensor(q[:, :, 5 * P:6 * P], cur[:, :, :], nxt[:, :, :], ALU.not_equal))
            v.wait_ge(s_c, 48)
            v.wait_ge(s_row, 32)
            link(nc.vector.memset(ones[:, :], 1.0))
            link(nc.vector.tensor_tensor_scan(out=run[:, :], data0=extra_row[:, :], data1=ones[:, :],
                                              initial=-1.0, op0=ALU.add, op1=ALU.add))
            nc.vector.tensor_tensor(pos[:, :], run[:, :], extra_row[:, :], ALU.subtract).then_inc(s_pos, 1)
            m.le_vec_n = link.n

        @block.sync
        def _(sp):
            sp.dma_start(cur[:, :, :], flat(1)).then_inc(s_in, 16)
            sp.dma_start(prev[:, :, :], flat(0)).then_inc(s_in, 16)
            sp.dma_start(nxt[:, :, :], flat(2)).then_inc(s_in, 16)
            sp.dma_start(srci[:, :, :], m.src.rearrange("(c p) e -> p c e", p=P)).then_inc(s_in, 16)
            sp.dma_start(q[:, :, 2 * P:3 * P], m.ew.rearrange("(c p) e -> p c e", p=P)).then_inc(s_w, 16)
            sp.dma_start(q[:, :, 3 * P:4 * P], m.ew2.rearrange("(c p) e -> p c e", p=P)).then_inc(s_w, 16)
            sp.dma_start(m.ident[:, :], m.c_ident).then_inc(s_c, 16)
            sp.dma_start(m.iota[:, :], m.c_iota).then_inc(s_c, 16)
            sp.dma_start(m.step_col[:, :], m.c_step).then_inc(s_c, 16)
            sp.wait_ge(s_ct, 1)
            sp.dma_start(m.d_extra.rearrange("(c p) -> c p", p=P), extraT[:, :]).then_inc(s_row, 16)
            sp.wait_ge(s_row, 16)
            sp.dma_start(extra_row[:, :], m.d_extra.rearrange("(a s) -> a s", a=1)).then_inc(s_row, 16)
            sp.wait_ge(s_pos, 1)
            sp.dma_start(m.d_pos.rearrange("(a s) -> a s", a=1), pos[:, :]).then_inc(s_posq, 16)
            sp.wait_ge(s_posq, 16)
            with nc.allow_non_contiguous_dma(reason="one column of the table"):
                sp.dma_start(q[:, :, QF * P:QF * P + 1],
                             m.d_pos.rearrange("(c p a) -> p c a", p=P, a=1)).then_inc(s_posq, 16)
            sp.wait_ge(s_posq, 32)
            sp.wait_ge(s_w, 32)
            sp.wait_ge(s_v, m.le_vec_n)
            sp.dma_start(m.d_q.rearrange("(c p) w -> p c w", p=P), q[:, :, :]).then_inc(s_q, 16)
            sp.wait_ge(s_q, 16)

        @block.tensor
        def _(pe):
            pe.wait_ge(s_c, 48)
            pe.wait_ge(s_v, 5)
            nc.tensor.transpose(ps[0:CHUNKS, 0:P], extra[:, :], m.ident[:, :]).then_inc(s_t, 1)


def place_steps(nc, m):
    with ExitStack() as ctx:
        sb = lambda name, shape, dt: ctx.enter_context(nc.sbuf_tensor(name, shape, dt))
        posb = sb("pos_all", [P, STEPS], fp32)
        junk = sb("junk", [P, STEPS], fp32)
        count = sb("tiles_begun", [P, CHUNKS], fp32)
        tile = sb("tile_of_step", [P, CHUNKS], fp32)
        tile_i = sb("tile_of_step_i", [P, CHUNKS], i32)
        g = sb("step_fields", [P, CHUNKS, QW], fp32)
        blk = sb("block_of_step", [P, CHUNKS], fp32)
        base = sb("base_of_step", [P, CHUNKS], fp32)
        ok = sb("edge_is_mine", [P, CHUNKS, P], fp32)
        low = sb("low_side", [P, CHUNKS, P], fp32)
        rows = sb("tile_block_rows", [CHUNKS, 2, P], fp32)
        rowf = sb("tile_block_row", [1, 2, STEPS], fp32)
        s_b, s_v, s_ti, s_g, s_ps, s_free, s_rows, s_out, s_row = (
            m.sem(n) for n in ("st_pos", "st_vec", "st_tile", "st_rows_in", "st_psum",
                                            "st_copied", "st_rows", "st_out", "st_row"))
        FIELDS = ((0, m.dstS), (1, m.srcS), (2, m.ewS), (3, m.ew2S))
        block = ctx.enter_context(nc.Block())

        @block.vector
        def _(v):
            link = Chain(v, s_v)
            for t in (m.dstS, m.srcS, m.ewS, m.ew2S, m.weightS):
                nc.vector.memset(t[:, STEPS:], 0.0)
            v.wait_ge(s_b, 16)
            for j in range(CHUNKS):
                link(nc.vector.tensor_scalar(junk[:, :], posb[:, :], m.step_col[:, j:j + 1], None,
                                             ALU.is_le, ALU.add, accum_out=count[:, j:j + 1]))
            link(nc.vector.tensor_scalar(tile[:, :], count[:, :], 1.0, None, ALU.subtract))
            nc.vector.tensor_copy(tile_i[:, :], tile[:, :]).then_inc(s_ti, 1)
            v.wait_ge(s_g, 16 * CHUNKS)
            link(nc.vector.tensor_tensor(blk[:, :], m.step_col[:, :], g[:, :, QF * P], ALU.subtract))
            link(nc.vector.tensor_tensor(blk[:, :], blk[:, :], g[:, :, QF * P + 1], ALU.add))
            link(nc.vector.tensor_scalar(base[:, :], blk[:, :], float(P), None, ALU.mult))
            link(nc.vector.tensor_tensor(g[:, :, 0:P], g[:, :, 0:P], bc_last(base[:, :], P), ALU.subtract))
            link(nc.vector.tensor_scalar(blk[:, :], blk[:, :], float(BLOCKS - 1), None, ALU.min))
            m.st_local = link.n
            link(nc.vector.tensor_scalar(low[:, :, :], g[:, :, 0:P], 0.0, None, ALU.is_ge))
            link(nc.vector.scalar_tensor_tensor(ok[:, :, :], g[:, :, 0:P], float(P), low[:, :, :],
                                                ALU.is_lt, ALU.mult))
            for j in range(CHUNKS):
                for f, dst in FIELDS:
                    n = len(FIELDS) * j + f
                    v.wait_ge(s_ps, n + 1)
                    nc.vector.tensor_copy(dst[:, j * P:(j + 1) * P],
                                          m.ps[f % 2][f // 2][:, 0:P]).then_inc(s_free, 1)
            for a in range(2):
                v.wait_ge(s_ps, len(FIELDS) * CHUNKS + a + 1)
                nc.vector.tensor_copy(rows[:, a, :], m.ps[a][2][0:CHUNKS, 0:P]).then_inc(s_rows, 1)
            for f in (4, 5):
                link(nc.vector.scalar_tensor_tensor(g[:, :, f * P:(f + 1) * P], ok[:, :, :], FAR,
                                                    g[:, :, f * P:(f + 1) * P], ALU.mult, ALU.mult))
            link(nc.vector.tensor_tensor(g[:, :, 0:P], g[:, :, 2 * P:3 * P], ok[:, :, :], ALU.mult))
            link(nc.vector.tensor_scalar(low[:, :, :], ok[:, :, :], 1.0, -FAR, ALU.subtract, ALU.mult))
            link(nc.vector.tensor_tensor(g[:, :, 0:P], g[:, :, 0:P], low[:, :, :], ALU.add))
            m.st_masked = link.n
            v.wait_ge(s_row, 32)
            nc.vector.tensor_scalar(m.tile_row[:, :], rowf[:, 0, :], float(P), None, ALU.mult)
            nc.vector.memset(m.off_row[:, 0:2 * UNIT], 0)
            nc.vector.tensor_scalar(m.off_row[:, 2 * UNIT:], rowf[:, 1, :], float(P), None, ALU.mult)

        @block.sync
        def _(sp):
            sp.dma_start(posb[:, :], m.d_pos.partition_broadcast(P)).then_inc(s_b, 16)
            sp.wait_ge(s_v, m.st_masked)
            for f, dst in ((4, m.d_start), (5, m.d_end), (0, m.d_ewm), (2, m.d_ew[0])):
                sp.dma_start(dst.rearrange("(c p e) -> p c e", p=P, e=P),
                             g[:, :, f * P:(f + 1) * P]).then_inc(s_out, 16)
            sp.dma_start(m.d_mine.rearrange("(c p e) -> p c e", p=P, e=P), ok[:, :, :]).then_inc(s_out, 16)
            sp.wait_ge(s_rows, 2)
            sp.dma_start(m.d_tb.rearrange("a (c p) -> c a p", p=P), rows[:, :, :]).then_inc(s_row, 16)
            sp.wait_ge(s_row, 16)
            sp.dma_start(rowf[:, :, :], m.d_tb.rearrange("(o a) s -> o a s", o=1)).then_inc(s_row, 16)
            sp.wait_ge(s_out, 80)

        @block.gpsimd
        def _(pool):
            pool.wait_ge(s_ti, 1)
            for j in range(CHUNKS):
                nc.gpsimd.indirect_dma_start(g[:, j, :], None, m.d_q,
                                             bass.IndirectOffsetOnAxis(ap=tile_i[:, j:j + 1], axis=0)
                                             ).then_inc(s_g, 16)

        @block.tensor
        def _(pe):
            pe.wait_ge(s_v, m.st_local)
            for j in range(CHUNKS):
                for f, dst in FIELDS:
                    n = len(FIELDS) * j + f
                    if j:
                        pe.wait_ge(s_free, n + 1 - len(FIELDS))
                    nc.tensor.transpose(m.ps[f % 2][f // 2][:, 0:P], g[:, j, f * P:(f + 1) * P],
                                        m.ident[:, :]).then_inc(s_ps, 1)
            for a, src in enumerate((tile, blk)):
                nc.tensor.transpose(m.ps[a][2][0:CHUNKS, 0:P], src[:, :], m.ident[:, :]).then_inc(s_ps, 1)


def edge_softmax(nc, m, tag, dest, score=None, floor=None):
    with ExitStack() as ctx:
        sb = lambda name, shape, dt=fp32: ctx.enter_context(nc.sbuf_tensor(tag + name, shape, dt))
        val = sb("val", [P, STEPS])
        fwd = sb("fwd", [P, STEPS])
        both = sb("both", [P, STEPS])
        start = sb("start", [P, STEPS])
        end = sb("end", [P, STEPS])
        mine = sb("mine", [P, STEPS])
        rows = sb("rows", [P, CHUNKS, P])
        tail = [sb(f"tail{i}", [P, 2]) for i in range(2)]
        tail_row = [sb(f"tail_row{i}", [1, 2, P]) for i in range(2)]
        carry_row = [sb(f"carry_row{i}", [1, P + 1]) for i in range(2)]
        carry = [sb(f"carry{i}", [P, 1]) for i in range(2)]
        s_ps, s_free, s_rows, s_val, s_in, s_v, s_t, s_e, s_w, s_r = (
            m.sem(tag + n) for n in ("pe", "copied", "rows_out", "val_in", "marks_in", "vec",
                                                  "carries", "exp", "w_out", "w_rows"))
        run = lambda d: d.rearrange("(p s) -> p s", p=P)
        bank = lambda j: m.ps[j % 2][j // 2 % 4]
        block = ctx.enter_context(nc.Block())
        at = {}

        @block.vector
        def _(v):
            link = Chain(v, s_v)
            n = 0
            if score is not None:
                for j in range(CHUNKS):
                    v.wait_ge(s_ps, j + 1)
                    nc.vector.tensor_copy(rows[:, j, :], bank(j)[:, 0:P]).then_inc(s_free, 1)
            v.wait_ge(s_in, 48)
            v.wait_ge(s_val, 32 if score is not None else 16)
            for i in range(2):
                link(nc.vector.memset(carry_row[i][:, :], FAR))
            if score is not None:
                link(nc.vector.tensor_tensor(val[:, :], val[:, :], mine[:, :], ALU.mult))
                link(nc.vector.tensor_scalar(mine[:, :], mine[:, :], 1.0, -FAR, ALU.subtract, ALU.mult))
                link(nc.vector.tensor_tensor(val[:, :], val[:, :], mine[:, :], ALU.add))
            for i, (marks, src, out) in enumerate(((start, val, fwd), (end, fwd, both))):
                way = slice(None, None, -1 if i else 1)
                scan = lambda first: nc.vector.tensor_tensor_scan(
                    out=out[:, way], data0=marks[:, way], data1=src[:, way], initial=first,
                    op0=ALU.add, op1=ALU.max)
                link(scan(FAR))
                edge = 0 if i else STEPS - 1
                link(nc.vector.tensor_reduce(tail[i][:, 0:1], marks[:, :], AX.X, ALU.min))
                link(nc.vector.tensor_copy(tail[i][:, 1:2], out[:, edge:edge + 1]))
                at["tail", i] = link.n
                v.wait_ge(s_t, 64 * i + 32)
                into = carry_row[i][:, P - 1::-1] if i else carry_row[i][:, 1:P + 1]
                link(nc.vector.tensor_tensor_scan(out=into, data0=tail_row[i][:, 0, way],
                                                  data1=tail_row[i][:, 1, way], initial=FAR,
                                                  op0=ALU.add, op1=ALU.max))
                at["carry", i] = link.n
                v.wait_ge(s_t, 64 * i + 64)
                link(scan(carry[i][:, 0:1]))
            if floor is not None:
                link(nc.vector.tensor_scalar(both[:, :], both[:, :], floor, None, ALU.max))
            link(nc.vector.tensor_tensor(val[:, :], val[:, :], both[:, :], ALU.subtract))
            link(nc.vector.tensor_scalar(val[:, :], val[:, :], -200.0, None, ALU.max))
            at["arg"] = link.n
            base = CHUNKS if score is not None else 0
            for j in range(CHUNKS):
                v.wait_ge(s_ps, base + j + 1)
                nc.vector.tensor_copy(dest[:, j * P:(j + 1) * P], bank(j)[:, 0:P]).then_inc(s_free, 1)

        @block.sync
        def _(sp):
            for t, d in ((start, m.d_start), (end, m.d_end), (mine, m.d_mine)):
                sp.dma_start(t[:, :], run(d)).then_inc(s_in, 16)
            if score is not None:
                sp.wait_ge(s_free, CHUNKS)
                sp.dma_start(m.d_score.rearrange("(c p e) -> p c e", p=P, e=P), rows[:, :, :]).then_inc(s_val, 16)
                sp.wait_ge(s_val, 16)
                sp.dma_start(val[:, :], run(m.d_score)).then_inc(s_val, 16)
            else:
                sp.dma_start(val[:, :], run(m.d_ewm)).then_inc(s_val, 16)
            with nc.allow_non_contiguous_dma(reason="one value per partition"):
                for i in range(2):
                    sp.wait_ge(s_v, at["tail", i])
                    sp.dma_start(m.d_tail[i].rearrange("a (p o) -> p a o", o=1), tail[i][:, :].unsqueeze(2)).then_inc(s_t, 16)
                    sp.wait_ge(s_t, 64 * i + 16)
                    sp.dma_start(tail_row[i][:, :, :], m.d_tail[i:i + 1]).then_inc(s_t, 16)
                    sp.wait_ge(s_v, at["carry", i])
                    sp.dma_start(m.d_carry[i:i + 1], carry_row[i][:, i:P + i]).then_inc(s_t, 16)
                    sp.wait_ge(s_t, 64 * i + 48)
                    sp.dma_start(carry[i][:, :], m.d_carry[i].rearrange("(p o) -> p o", o=1)).then_inc(s_t, 16)
            sp.wait_ge(s_e, 1)
            sp.dma_start(run(m.d_weight), val[:, :]).then_inc(s_w, 16)
            sp.wait_ge(s_w, 16)
            sp.dma_start(rows[:, :, :], m.d_weight.rearrange("(c p e) -> p c e", p=P, e=P)).then_inc(s_r, 16)

        @block.scalar
        def _(act):
            act.wait_ge(s_v, at["arg"])
            nc.scalar.activation(val[:, :], val[:, :], ACT.Exp).then_inc(s_e, 1)

        @block.tensor
        def _(pe):
            if score is not None:
                for j in range(CHUNKS):
                    if j >= 8:
                        pe.wait_ge(s_free, j - 7)
                    nc.tensor.transpose(bank(j)[:, 0:P], score[:, j * P:(j + 1) * P], m.ident[:, :]).then_inc(s_ps, 1)
            base = CHUNKS if score is not None else 0
            pe.wait_ge(s_r, 16)
            if base:
                pe.wait_ge(s_free, base)
            for j in range(CHUNKS):
                if j >= 8:
                    pe.wait_ge(s_free, base + j - 7)
                nc.tensor.transpose(bank(j)[:, 0:P], rows[:, j, :], m.ident[:, :]).then_inc(s_ps, 1)


def store_table(nc, m, tag, tile, table):
    s_out = m.sem(tag + "table_out")
    with nc.Block() as block:
        @block.sync
        def _(sp):
            sp.dma_start(table.rearrange("(b p) w -> p b w", p=P), tile[:, :, :]).then_inc(s_out, 16)
            sp.wait_ge(s_out, 16)


class Semaphores:

    def __init__(self, nc):
        self.nc, self.out = nc, []

    def __call__(self, name):
        self.out.append(self.nc.alloc_semaphore(name))
        return self.out[-1]

    def clear(self):
        self.nc.clear_and_free_semaphores(self.out)
        self.nc.all_engine_barrier()
        self.out = []


class Ticks:

    def __init__(self, sem, trip, per):
        self.sem, self.trip, self.per, self.n = sem, trip, per, 0

    def __call__(self, ins):
        self.n += 1
        ins.then_inc(self.sem, 1)
        return self.trip * self.per + self.n


def block_offsets(nc, m, step, engine):
    _, regs = nc.values_load_multi_w_load_instructions(
        m.off_row[0:1, bass.ds(step, UNIT)], engines=(engine,), min_val=0, max_val=(BLOCKS - 1) * P,
        skip_runtime_bounds_check_because="place_steps clamps the blocks to those that exist")
    return regs


def begin_sums(nc, m, v, s_added):
    for u in range(2):
        nc.vector.memset(m.ps[u][3][:, :], 0.0)
    nc.vector.memset(m.acc[:, :], 0.0).then_inc(s_added, 1)


def add_sums(nc, m, v, step, sums, width, s_added):
    offsets = block_offsets(nc, m, step, mybir.EngineType.DVE)
    for k in range(UNIT):
        into = m.acc[:, bass.ds(offsets[k], width)]
        v.wait_ge(s_added, step + (k + 1))
        nc.vector.tensor_tensor(into, into, sums[:, k * width:(k + 1) * width], ALU.add).then_inc(s_added, 1)


def added(unit):
    return UNIT * unit + (UNIT + 1)


def stage_unit(nc, m, act, unit, slot, idx, col, fields, s_free, s_staged):
    if s_free is not None:
        act.wait_ge(s_free, done(unit, UNITS))
    last = None
    if idx is not None:
        last = nc.scalar.copy(idx[:, slot, :], m.srcS[:, bass.ds(unit * UNIT, UNIT)])
    for f, tile in enumerate(fields):
        last = nc.scalar.copy(col[:, slot, f, :], tile[:, bass.ds(unit * UNIT, UNIT)])
    last.then_inc(s_staged, 1)


def stage_first(nc, m, act, idx, col, fields, s_staged):
    act.sem_inc(s_staged, CREDIT)
    for n in range(LEAD):
        stage_unit(nc, m, act, n, n, idx, col, fields, None, s_staged)


def gather_rows(nc, m, pool, idx, g, cols, table, s_staged, gathered):
    with nc.gpsimd.Fori(0, TRIPS) as i:
        for q in range(UNITS):
            pool.wait_ge(s_staged, done(i * UNITS + q))
            nc.gpsimd.nop(nofuse=True)
            for k in range(UNIT):
                nc.gpsimd.indirect_dma_start(
                    g[:, q, k, 0:cols], None, table,
                    bass.IndirectOffsetOnAxis(ap=idx[:, q, k:k + 1], axis=0)).then_inc(gathered[q], 16)


def weighted_sum(nc, m, tag, weight, width, table=None, stored=None):
    with ExitStack() as ctx:
        sb = lambda name, shape, dt=fp32: ctx.enter_context(nc.sbuf_tensor(tag + name, shape, dt))
        g = sb("rows", [P, UNITS, UNIT, width])
        idx = sb("idx", [P, UNITS, UNIT], i32) if table is not None else None
        col = sb("columns", [P, UNITS, 2, UNIT])
        oh = sb("onehot", [P, 2, UNIT, P])
        gathered = [m.sem(f"{tag}gathered{q}") for q in range(UNITS)]
        s_staged, s_oh, s_sum, s_add = (m.sem(tag + n) for n in
                                        ("staged", "onehot_ready", "summed", "added"))
        per = 16 * UNIT if table is not None else 16
        fields = (m.dstS, weight)
        block = ctx.enter_context(nc.Block())

        @block.vector
        def _(v):
            v.sem_inc(s_oh, CREDIT)
            begin_sums(nc, m, v, s_add)
            with nc.vector.Fori(0, TRIPS) as i:
                for q in range(UNITS):
                    n, u = i * UNITS + q, q % 2
                    v.wait_ge(s_staged, done(n))
                    v.wait_ge(s_sum, done(n, 2))
                    for k in range(UNIT):
                        last = nc.vector.tensor_scalar(oh[:, u, k, :], m.iota[:, :], col[:, q, 0, k:k + 1],
                                                       col[:, q, 1, k:k + 1], ALU.is_equal, ALU.mult)
                    last.then_inc(s_oh, 1)
                    add_sums(nc, m, v, n * UNIT, m.ps[u][3], width, s_add)
            for n in (TRIPS * UNITS, TRIPS * UNITS + 1):
                v.wait_ge(s_sum, done(n, 2))
                add_sums(nc, m, v, n * UNIT, m.ps[n % 2][3], width, s_add)

        @block.tensor
        def _(pe):
            pe.sem_inc(s_sum, CREDIT)
            with nc.tensor.Fori(0, TRIPS) as i:
                for q in range(UNITS):
                    n, u = i * UNITS + q, q % 2
                    pe.wait_ge(s_oh, done(n))
                    pe.wait_ge(gathered[q], per * i + per)
                    pe.wait_ge(s_add, added(n))
                    for k in range(UNIT):
                        last = nc.tensor.matmul(m.ps[u][3][:, k * width:(k + 1) * width], oh[:, u, k, :],
                                                g[:, q, k, :], start=True, stop=True)
                    last.then_inc(s_sum, 1)

        @block.scalar
        def _(act):
            stage_first(nc, m, act, idx, col, fields, s_staged)
            with nc.scalar.Fori(0, TRIPS) as i:
                for q in range(UNITS):
                    stage_unit(nc, m, act, i * UNITS + (q + LEAD), (q + LEAD) % UNITS, idx, col, fields,
                               s_sum, s_staged)

        if table is not None:
            @block.gpsimd
            def _(pool):
                gather_rows(nc, m, pool, idx, g, width, table, s_staged, gathered)
        else:
            @block.sync
            def _(sp):
                with nc.sync.Fori(0, TRIPS) as i:
                    for q in range(UNITS):
                        n = i * UNITS + q
                        sp.wait_ge(s_sum, done(n, UNITS))
                        sp.dma_start(g[:, q, :, :].rearrange("p k w -> p (k w)"),
                                     stored[bass.ds(n * P, P), :]).then_inc(gathered[q], 16)


def layer0_edges(nc, m):
    with ExitStack() as ctx:
        sb = lambda name, shape, dt=fp32: ctx.enter_context(nc.sbuf_tensor("l0" + name, shape, dt))
        g = sb("rows", [P, UNITS, UNIT, D])
        idx = sb("idx", [P, UNITS, UNIT], i32)
        col = sb("columns", [P, UNITS, 3, UNIT])
        dist = sb("dist", [1, UNITS, UNIT * P])
        oh = sb("onehot", [P, 2, UNIT, P])
        ohT = sb("onehotT", [P, 2, UNIT * P])
        hid = sb("hidden", [D + 1, 2, UNIT * P])
        above = sb("above", [P, 2, UNIT, BINS])
        below = sb("below", [P, 2, UNIT, BINS])
        diff = sb("diff", [P, 2, UNIT * D])
        size = sb("size", [P, 2, UNIT * D])
        keep = sb("keep", [P, 2, UNIT * D])
        powr = sb("power", [P, 2, UNIT * D])
        padw = sb("padded", [P, 2, UNIT, D])
        val = sb("values", [P, 2, UNIT, 2 * D])
        gathered = [m.sem(f"l0gathered{q}") for q in range(UNITS)]
        came = [m.sem(f"l0dist{q}") for q in range(UNITS)]
        (s_staged, s_oh, s_t, s_tc, s_h, s_hc, s_m, s_hd, s_size, s_pow, s_val, s_sum, s_add, s_v,
         s_one, s_ln) = (m.sem("l0" + n) for n in
                         ("staged", "onehot_ready", "onehot_turned", "turned_copied", "hidden_ready",
                          "hidden_copied", "mlp_ready", "dst_rows_ready", "size_ready", "power_ready",
                          "values_ready", "summed", "added", "vec", "ones", "ln"))
        fields = (m.dstS, m.ewS, m.ew2S)
        flat = lambda t, u: t[:, u, :, :].rearrange("p k w -> p (k w)")
        PER = 8 * UNITS
        block = ctx.enter_context(nc.Block())

        @block.vector
        def _(v):
            nc.vector.memset(hid[D:D + 1, :, :], 1.0).then_inc(s_one, 1)
            for s in (s_oh, s_size, s_val):
                v.sem_inc(s, CREDIT)
            begin_sums(nc, m, v, s_add)
            with nc.vector.Fori(0, TRIPS) as i:
                tick = Ticks(s_v, i, PER)
                for q0 in range(0, UNITS, 2):
                    pair = [(q0 + u, u, i * UNITS + (q0 + u)) for u in range(2)]
                    for q, u, n in pair:
                        v.wait_ge(s_staged, done(n))
                        v.wait_ge(s_sum, done(n, 2))
                        for k in range(UNIT):
                            last = nc.vector.tensor_scalar(oh[:, u, k, :], m.iota[:, :],
                                                           col[:, q, 0, k:k + 1], None, ALU.is_equal)
                        last.then_inc(s_oh, 1)
                    at = {}
                    for q, u, n in pair:
                        d = bc_last(col[:, q, 1, :], BINS)
                        tick(nc.vector.tensor_tensor(above[:, u, :, :], bc_mid(m.bins[:, 0:BINS], UNIT), d,
                                                     ALU.subtract))
                        at[u] = tick(nc.vector.tensor_tensor(below[:, u, :, :], d,
                                                             bc_mid(m.bins[:, 1:BINS + 1], UNIT), ALU.subtract))
                    for q, u, n in pair:
                        v.wait_ge(s_v, at[u])
                        at[u] = tick(nc.vector.tensor_tensor(above[:, u, :, :], above[:, u, :, :],
                                                             below[:, u, :, :], ALU.mult))
                    for q, u, n in pair:
                        add_sums(nc, m, v, n * UNIT, m.ps[u][3], 2 * D, s_add)
                    for q, u, n in pair:
                        v.wait_ge(s_v, at[u])
                        tick(nc.vector.tensor_scalar(val[:, u, :, 0:BINS], above[:, u, :, :], 0.0, None,
                                                     ALU.is_gt))
                    for q, u, n in pair:
                        v.wait_ge(s_m, done(n))
                        mlp = m.ps[u][1][:, 0:UNIT * BINS].rearrange("p (k w) -> p k w", w=BINS)
                        at[u] = tick(nc.vector.tensor_scalar(val[:, u, :, BINS:D], mlp, 0.0, None, ALU.max))
                    for q, u, n in pair:
                        v.wait_ge(s_v, at[u])
                        tick(nc.vector.tensor_tensor(padw[:, u, :, :], val[:, u, :, 0:D],
                                                     bc_last(col[:, q, 2, :], D), ALU.mult))
                    for q, u, n in pair:
                        v.wait_ge(s_hd, done(n))
                        v.wait_ge(gathered[q], 16 * UNIT * i + 16 * UNIT)
                        at[u] = tick(nc.vector.scalar_tensor_tensor(
                            diff[:, u, :], flat(g, q), m.na[:, 0:1], m.ps[u][2][:, 0:UNIT * D],
                            ALU.mult, ALU.add))
                    for q, u, n in pair:
                        v.wait_ge(s_v, at[u])
                        nc.vector.scalar_tensor_tensor(size[:, u, :], diff[:, u, :], -1.0, diff[:, u, :],
                                                       ALU.mult, ALU.max).then_inc(s_size, 1)
                    for q, u, n in pair:
                        at[u] = tick(nc.vector.tensor_scalar(keep[:, u, :], diff[:, u, :], 0.0, m.b0[:, 0:1],
                                                             ALU.not_equal, ALU.max))
                    for q, u, n in pair:
                        v.wait_ge(s_v, at[u])
                        nc.vector.tensor_tensor(keep[:, u, :], keep[:, u, :], flat(padw, u),
                                                ALU.mult).then_inc(s_one, 1)
                    for q, u, n in pair:
                        v.wait_ge(s_one, n + 2)
                        v.wait_ge(s_pow, done(n))
                        nc.vector.tensor_tensor(val[:, u, :, D:2 * D],
                                                powr[:, u, :].rearrange("p (k w) -> p k w", w=D),
                                                keep[:, u, :].rearrange("p (k w) -> p k w", w=D),
                                                ALU.mult).then_inc(s_val, 1)
                assert tick.n == PER
            for n in (TRIPS * UNITS, TRIPS * UNITS + 1):
                v.wait_ge(s_sum, done(n, 2))
                add_sums(nc, m, v, n * UNIT, m.ps[n % 2][3], 2 * D, s_add)

        @block.tensor
        def _(pe):
            for s in (s_t, s_h, s_m, s_hd, s_sum):
                pe.sem_inc(s, CREDIT)
            pe.wait_ge(s_one, 1)
            with nc.tensor.Fori(0, TRIPS) as i:
                for q0 in range(0, UNITS, 2):
                    pair = [(q0 + u, u, i * UNITS + (q0 + u)) for u in range(2)]
                    for q, u, n in pair:
                        pe.wait_ge(came[q], 16 * i + 16)
                        pe.wait_ge(s_hc, done(n, 2))
                        nc.tensor.matmul(m.ps[u][2][0:D, :], m.w1[:, :], dist[0:1, q, :], start=True,
                                         stop=True).then_inc(s_h, 1)
                    for q, u, n in pair:
                        pe.wait_ge(s_oh, done(n))
                        pe.wait_ge(s_tc, done(n, 2))
                        for k in range(UNIT):
                            last = nc.tensor.transpose(m.ps[u][0][:, k * P:(k + 1) * P], oh[:, u, k, :],
                                                       m.ident[:, :])
                        last.then_inc(s_t, 1)
                    for q, u, n in pair:
                        pe.wait_ge(s_hc, done(n))
                        for k in range(UNIT):
                            c = k * BINS
                            last = nc.tensor.matmul(m.ps[u][1][:, c:c + BINS], hid[:, u, k * P:(k + 1) * P],
                                                    m.w2b[:, :], start=True, stop=True)
                        last.then_inc(s_m, 1)
                    for q, u, n in pair:
                        pe.wait_ge(s_tc, done(n))
                        offsets = block_offsets(nc, m, (n + 2) * UNIT, mybir.EngineType.PE)
                        for k in range(UNIT):
                            last = nc.tensor.matmul(m.ps[u][2][:, k * D:(k + 1) * D], ohT[:, u, k * P:(k + 1) * P],
                                                    m.xb[:, bass.ds(offsets[k], D)], start=True, stop=True)
                        last.then_inc(s_hd, 1)
                    for q, u, n in pair:
                        pe.wait_ge(s_val, done(n))
                        pe.wait_ge(s_add, added(n))
                        for k in range(UNIT):
                            last = nc.tensor.matmul(m.ps[u][3][:, k * 2 * D:(k + 1) * 2 * D], oh[:, u, k, :],
                                                    val[:, u, k, :], start=True, stop=True)
                        last.then_inc(s_sum, 1)

        @block.scalar
        def _(act):
            for s in (s_tc, s_hc, s_pow):
                act.sem_inc(s, CREDIT)
            stage_first(nc, m, act, idx, col, fields, s_staged)
            with nc.scalar.Fori(0, TRIPS) as i:
                for q0 in range(0, UNITS, 2):
                    pair = [(q0 + u, u, i * UNITS + (q0 + u)) for u in range(2)]
                    for q, u, n in pair:
                        stage_unit(nc, m, act, n + LEAD, (q + LEAD) % UNITS, idx, col, fields, s_sum, s_staged)
                    for q, u, n in pair:
                        act.wait_ge(s_h, done(n))
                        act.wait_ge(s_m, done(n, 2))
                        nc.scalar.activation(hid[0:D, u, :], m.ps[u][2][0:D, :], ACT.Relu,
                                             bias=m.b1[:, 0:1]).then_inc(s_hc, 1)
                    for q, u, n in pair:
                        act.wait_ge(s_t, done(n))
                        act.wait_ge(s_hd, done(n, 2))
                        nc.scalar.copy(ohT[:, u, :], m.ps[u][0][:, :]).then_inc(s_tc, 1)
                    for q, u, n in pair:
                        act.wait_ge(s_size, done(n))
                        nc.scalar.activation(size[:, u, :], size[:, u, :], ACT.Ln,
                                             bias=m.tiny[:, 0:1]).then_inc(s_ln, 1)
                    for q, u, n in pair:
                        act.wait_ge(s_ln, n + 1)
                        nc.scalar.activation(powr[:, u, :], size[:, u, :], ACT.Exp,
                                             scale=m.b[:, 0:1]).then_inc(s_pow, 1)

        @block.gpsimd
        def _(pool):
            gather_rows(nc, m, pool, idx, g, D, m.x, s_staged, gathered)

        @block.sync
        def _(sp):
            with nc.sync.Fori(0, TRIPS) as i:
                for q in range(UNITS):
                    n = i * UNITS + q
                    sp.wait_ge(s_sum, done(n, UNITS))
                    sp.dma_start(dist[0:1, q, :], m.d_ew[:, bass.ds(n * UNIT * P, UNIT * P)]).then_inc(came[q], 16)


def project(nc, m, tag, width, w, out):
    with ExitStack() as ctx:
        sb = lambda name, shape, dt=fp32: ctx.enter_context(nc.sbuf_tensor(tag + name, shape, dt))
        part = sb("group", [P, GROUP * P])
        turned = sb("group_turned", [P, GROUP * P])
        s_in, s_t, s_tc, s_p, s_out = (m.sem(tag + n) for n in
                                       ("in", "turned", "turned_copied", "product", "out"))
        cut = ((0, 4), (4, GROUP))
        block = ctx.enter_context(nc.Block())

        @block.scalar
        def _(act):
            act.sem_inc(s_in, CREDIT)
            act.sem_inc(s_tc, CREDIT)
            with nc.scalar.Fori(0, BLOCKS // GROUP) as i:
                act.wait_ge(s_t, done(i, 1))
                nc.scalar.copy(part[:, :], m.acc[:, bass.ds(i * GROUP * P, GROUP * P)]).then_inc(s_in, 1)
                act.wait_ge(s_t, done(i))
                act.wait_ge(s_p, done(i, 1))
                nc.scalar.copy(turned[0:width, 0:4 * P], m.ps[0][0][0:width, :])
                nc.scalar.copy(turned[0:width, 4 * P:GROUP * P],
                               m.ps[0][1][0:width, 0:(GROUP - 4) * P]).then_inc(s_tc, 1)

        @block.tensor
        def _(pe):
            pe.sem_inc(s_t, CREDIT)
            pe.sem_inc(s_p, CREDIT)
            with nc.tensor.Fori(0, BLOCKS // GROUP) as i:
                pe.wait_ge(s_in, done(i))
                pe.wait_ge(s_tc, done(i, 1))
                for k in range(GROUP):
                    last = nc.tensor.transpose(m.ps[0][k // 4][0:width, k % 4 * P:(k % 4 + 1) * P],
                                               part[:, k * P:k * P + width], m.ident[:, :])
                last.then_inc(s_t, 1)
                pe.wait_ge(s_tc, done(i))
                pe.wait_ge(s_out, done(i, 1))
                for k in range(GROUP):
                    last = nc.tensor.matmul(m.ps[1][0][:, k * D:(k + 1) * D],
                                            turned[0:width, k * P:(k + 1) * P], w[0:width, :],
                                            start=True, stop=True)
                last.then_inc(s_p, 1)

        @block.vector
        def _(v):
            v.sem_inc(s_out, CREDIT)
            with nc.vector.Fori(0, BLOCKS // GROUP) as i:
                v.wait_ge(s_p, done(i))
                nc.vector.tensor_copy(out[:, bass.ds(i * GROUP * D, GROUP * D)],
                                      m.ps[1][0][:, 0:GROUP * D]).then_inc(s_out, 1)


def layer_norm(nc, m, tag, y):
    with ExitStack() as ctx:
        sb = lambda name, shape, dt=fp32: ctx.enter_context(nc.sbuf_tensor(tag + name, shape, dt))
        mean = sb("mean", [P, BLOCKS])
        sq = sb("squares", [P, BLOCKS * D])
        var = sb("var", [P, BLOCKS])
        dev = sb("dev", [P, BLOCKS])
        s_v, s_d = (m.sem(tag + n) for n in ("vec", "dev"))
        wide = lambda t: t[:, :].rearrange("p (b d) -> p b d", d=D)
        block = ctx.enter_context(nc.Block())

        @block.vector
        def _(v):
            link = Chain(v, s_v)
            link(nc.vector.tensor_reduce(mean[:, :], wide(y), AX.X, ALU.add))
            link(nc.vector.tensor_scalar(mean[:, :], mean[:, :], 1.0 / D, None, ALU.mult))
            link(nc.vector.tensor_tensor(wide(y), wide(y), bc_last(mean[:, :], D), ALU.subtract))
            link(nc.vector.tensor_tensor(sq[:, :], y[:, :], y[:, :], ALU.mult))
            link(nc.vector.tensor_reduce(var[:, :], wide(sq), AX.X, ALU.add))
            link(nc.vector.tensor_scalar(var[:, :], var[:, :], 1.0 / D, 1e-5, ALU.mult, ALU.add))
            m.ln_n = link.n
            v.wait_ge(s_d, 1)
            link(nc.vector.reciprocal(dev[:, :], dev[:, :]))
            nc.vector.tensor_tensor(wide(m.xs), wide(y), bc_last(dev[:, :], D), ALU.mult)

        @block.scalar
        def _(act):
            act.wait_ge(s_v, m.ln_n)
            nc.scalar.activation(dev[:, :], var[:, :], ACT.Sqrt).then_inc(s_d, 1)


def node_view(tile, width=P):
    return tile[:, :].rearrange("p (b w) -> p b w", w=width)


def layer0_nodes_before(nc, m):
    s_in, s_v, s_z = (m.sem(n) for n in ("l0w_in", "l0w_vec", "l0w_zero"))
    block_ctx = ExitStack()
    with block_ctx:
        raw = block_ctx.enter_context(nc.sbuf_tensor("l0w_ab", [P, 2], fp32))
        block = block_ctx.enter_context(nc.Block())

        @block.sync
        def _(sp):
            sp.dma_start(node_view(m.xs, D), m.x.rearrange("(b p) d -> p b d", p=P)).then_inc(s_in, 16)
            sp.dma_start(m.w1[:, :], m.L0_gnn_mlp_w1).then_inc(s_in, 16)
            sp.dma_start(m.b1[:, :], m.L0_gnn_mlp_b1.rearrange("(d o) -> d o", o=1)).then_inc(s_in, 16)
            sp.dma_start(m.w2b[0:D, :], m.L0_gnn_mlp_w2).then_inc(s_in, 16)
            sp.dma_start(m.w2b[D:D + 1, :], m.L0_gnn_mlp_b2.rearrange("(o d) -> o d", o=1)).then_inc(s_in, 16)
            sp.dma_start(raw[:, 0:1], m.L0_gnn_pd_a.partition_broadcast(P)).then_inc(s_in, 16)
            sp.dma_start(raw[:, 1:2], m.L0_gnn_pd_b.partition_broadcast(P)).then_inc(s_in, 16)
            sp.dma_start(m.bins[:, :], m.c_bins).then_inc(s_in, 16)
            sp.dma_start(m.gw[0:D, :], m.L0_gnn_gamma_self_w).then_inc(s_in, 16)
            sp.dma_start(m.gw[D:P, :], m.L0_gnn_gamma_gathered_w).then_inc(s_in, 16)
            sp.dma_start(m.gb[:, :], m.L0_gnn_gamma_gathered_b.partition_broadcast(P)).then_inc(s_in, 16)

        @block.vector
        def _(v):
            link = Chain(v, s_v)
            nc.vector.memset(m.wcat[:, :], 0.0)
            v.wait_ge(s_in, 176)
            link(nc.vector.tensor_scalar(m.a[:, :], raw[:, 0:1], 0.0, 1.0, ALU.max, ALU.min))
            link(nc.vector.scalar_tensor_tensor(m.b[:, :], raw[:, 1:2], -1.0, raw[:, 1:2], ALU.mult, ALU.max))
            nc.vector.memset(m.tiny[:, :], TINY)
            link(nc.vector.tensor_scalar(m.b0[:, :], m.b[:, :], 0.0, None, ALU.is_equal))
            link(nc.vector.tensor_scalar(m.na[:, :], m.a[:, :], 1.0, None, ALU.subtract))
            link(nc.vector.tensor_scalar(node_view(m.xb)[:, :, 0:D], node_view(m.xs, D), m.a[:, 0:1], None,
                                         ALU.mult))


def layer0_nodes_after(nc, m):
    with ExitStack() as ctx:
        y = ctx.enter_context(nc.sbuf_tensor("l0y", [P, BLOCKS * D], fp32))
        inv = ctx.enter_context(nc.sbuf_tensor("l0inv", [P, BLOCKS * D], fp32))
        s_v = m.sem("l0n_vec")
        s_v2 = m.sem("l0n_vec2")
        acc = node_view(m.acc)
        with nc.Block() as block:
            @block.vector
            def _(v):
                link = Chain(v, s_v)
                link(nc.vector.tensor_scalar(node_view(inv, D), acc[:, :, 0:D], 1e-5, None, ALU.add))
                link(nc.vector.reciprocal(inv[:, :], inv[:, :]))
                link(nc.vector.tensor_tensor(acc[:, :, D:P], acc[:, :, D:P], node_view(inv, D), ALU.mult))
                link(nc.vector.tensor_copy(acc[:, :, 0:D], node_view(m.xs, D)))
        project(nc, m, "l0p_", P, m.gw, y)
        with nc.Block() as block:
            @block.vector
            def _(v):
                link = Chain(v, s_v2)
                link(nc.vector.tensor_tensor(node_view(y, D), node_view(y, D), bc_mid(m.gb[:, :], BLOCKS),
                                             ALU.add))
                link(nc.vector.scalar_tensor_tensor(y[:, :], y[:, :], 0.0, m.xs[:, :], ALU.max, ALU.add))
        layer_norm(nc, m, "l0ln_", y)


def layer1_nodes_before(nc, m):
    with ExitStack() as ctx:
        sb = lambda name, shape, dt=fp32: ctx.enter_context(nc.sbuf_tensor("l1b" + name, shape, dt))
        wnT = sb("wnT", [D, D])
        weT = sb("weT", [D, ED])
        att = sb("att", [D, 3])
        wide = sb("att_wide", [D, 3, P])
        u = sb("through", [P, 2, D])
        prod = sb("prod", [P, BLOCKS * D])
        tab = sb("table", [P, BLOCKS, D + 2])
        zd = sb("dst_score", [P, BLOCKS])
        zdT = sb("dst_score_rows", [BLOCKS, P])
        s_in, s_v, s_p, s_t, s_c, s_out = (m.sem("l1b_" + n) for n in
                                           ("in", "vec", "product", "turned", "copied", "out"))
        at = {}
        block = ctx.enter_context(nc.Block())

        @block.vector
        def _(v):
            link = Chain(v, s_v)
            v.wait_ge(s_in, 16 * 7)
            for f in range(3):
                link(nc.vector.tensor_copy(wide[:, f, :], att[:, f:f + 1].to_broadcast([D, P])))
            at["wide"] = link.n
            v.wait_ge(s_p, 1)
            link(nc.vector.tensor_copy(u[:, 0, :], m.ps[0][0][:, 0:D]))
            link(nc.vector.tensor_copy(u[:, 1, :], m.ps[0][1][:, 0:D]))
            link(nc.vector.tensor_copy(m.ve[:, :], m.ps[0][2][:, 0:ED]))
            x = node_view(m.xs, D)
            for f, out in ((0, tab[:, :, D]), (1, zd[:, :])):
                link(nc.vector.tensor_tensor(node_view(prod, D), x, bc_mid(u[:, f, :], BLOCKS), ALU.mult))
                link(nc.vector.tensor_reduce(out, node_view(prod, D), AX.X, ALU.add))
            link(nc.vector.tensor_copy(tab[:, :, 0:D], x))
            link(nc.vector.memset(tab[:, :, D + 1:D + 2], 1.0))
            at["table"] = link.n
            v.wait_ge(s_t, 1)
            nc.vector.tensor_copy(zdT[:, :], m.ps[1][0][0:BLOCKS, 0:P]).then_inc(s_c, 1)

        @block.tensor
        def _(pe):
            pe.wait_ge(s_v, at["wide"])
            nc.tensor.matmul(m.ps[0][0][:, 0:D], wide[:, 0, :], wnT[:, :], start=True, stop=True)
            nc.tensor.matmul(m.ps[0][1][:, 0:D], wide[:, 1, :], wnT[:, :], start=True, stop=True)
            nc.tensor.matmul(m.ps[0][2][:, 0:ED], wide[:, 2, :], weT[:, :], start=True, stop=True).then_inc(s_p, 1)
            pe.wait_ge(s_v, at["table"])
            nc.tensor.transpose(m.ps[1][0][0:BLOCKS, 0:P], zd[:, :], m.ident[:, :]).then_inc(s_t, 1)

        @block.sync
        def _(sp):
            sp.dma_start(wnT[:, :], m.wnT).then_inc(s_in, 16)
            sp.dma_start(weT[:, :], m.weT).then_inc(s_in, 16)
            for f, a in enumerate((m.L1_gnn_att_src, m.L1_gnn_att_dst, m.L1_gnn_att_edge)):
                sp.dma_start(att[:, f:f + 1], a.rearrange("(d o) -> d o", o=1)).then_inc(s_in, 16)
            sp.dma_start(m.wcat[0:D, :], m.L1_gnn_Wn).then_inc(s_in, 16)
            sp.dma_start(m.wcat[D + 2:L1W, :], m.L1_gnn_We).then_inc(s_in, 16)
            sp.wait_ge(s_v, at["table"])
            sp.dma_start(m.table1.rearrange("(b p) w -> p b w", p=P), tab[:, :, :]).then_inc(s_out, 16)
            sp.wait_ge(s_c, 1)
            sp.dma_start(m.d_zd.rearrange("(b p) -> b p", p=P), zdT[:, :]).then_inc(s_out, 16)
            sp.wait_ge(s_out, 32)
            sp.dma_start(m.xb[:, :], m.d_zd.partition_broadcast(P)).then_inc(s_out, 16)
            sp.wait_ge(s_out, 48)


def layer1_scores(nc, m):
    with ExitStack() as ctx:
        sb = lambda name, shape, dt=fp32: ctx.enter_context(nc.sbuf_tensor("l1" + name, shape, dt))
        g = sb("rows", [P, UNITS, UNIT, L1W])
        idx = sb("idx", [P, UNITS, UNIT], i32)
        col = sb("columns", [P, UNITS, 1, UNIT])
        junk = sb("junk", [P, 2, UNIT, P])
        zd = sb("zd", [P, 2, UNIT])
        prod = sb("prod", [P, 2, UNIT, ED])
        se = sb("se", [P, 2, UNIT])
        gathered = [m.sem(f"l1gathered{q}") for q in range(UNITS)]
        attrs = [m.sem(f"l1attrs{q}") for q in range(UNITS)]
        stored = [m.sem(f"l1stored{q}") for q in range(UNITS)]
        s_staged, s_used, s_v = (m.sem("l1" + n) for n in ("staged", "used", "vec"))
        PER = (UNIT + 4) * UNITS
        block = ctx.enter_context(nc.Block())

        @block.vector
        def _(v):
            v.sem_inc(s_used, CREDIT)
            with nc.vector.Fori(0, TRIPS) as i:
                tick = Ticks(s_v, i, PER)
                for q in range(UNITS):
                    n, u = i * UNITS + q, q % 2
                    v.wait_ge(s_staged, done(n))
                    offsets = block_offsets(nc, m, (n + 2) * UNIT, mybir.EngineType.DVE)
                    for k in range(UNIT):
                        tick(nc.vector.scalar_tensor_tensor(
                            junk[:, u, k, :], m.iota[:, :], col[:, q, 0, k:k + 1],
                            m.xb[:, bass.ds(offsets[k], P)], ALU.is_equal, ALU.mult,
                            accum_out=zd[:, u, k:k + 1]))
                    v.wait_ge(attrs[q], 16 * UNIT * i + 16 * UNIT)
                    v.wait_ge(gathered[q], 16 * UNIT * i + 16 * UNIT)
                    v.wait_ge(s_v, tick(nc.vector.tensor_tensor(
                        prod[:, u, :, :], g[:, q, :, D + 2:L1W], bc_mid(m.ve[:, :], UNIT), ALU.mult)))
                    v.wait_ge(s_v, tick(nc.vector.tensor_reduce(se[:, u, :], prod[:, u, :, :], AX.X, ALU.add)))
                    v.wait_ge(s_v, tick(nc.vector.tensor_tensor(se[:, u, :], se[:, u, :], g[:, q, :, D], ALU.add)))
                    v.wait_ge(s_v, tick(nc.vector.tensor_tensor(se[:, u, :], se[:, u, :], zd[:, u, :], ALU.add)))
                    v.wait_ge(stored[q], 16 * i + 16)
                    nc.vector.scalar_tensor_tensor(m.scoreS[:, bass.ds(n * UNIT, UNIT)], se[:, u, :], 0.2,
                                                   se[:, u, :], ALU.mult, ALU.max).then_inc(s_used, 1)
                assert tick.n == PER

        @block.scalar
        def _(act):
            stage_first(nc, m, act, idx, col, (m.dstS,), s_staged)
            with nc.scalar.Fori(0, TRIPS) as i:
                for q in range(UNITS):
                    n = i * UNITS + q
                    stage_unit(nc, m, act, n + LEAD, (q + LEAD) % UNITS, idx, col, (m.dstS,), s_used, s_staged)
                    act.wait_ge(gathered[q], 16 * UNIT * i + 16 * UNIT)
                    act.wait_ge(attrs[q], 16 * UNIT * i + 16 * UNIT)
                    act.dma_start(m.d_rows[bass.ds(n * P, P), :],
                                  g[:, q, :, :].rearrange("p k w -> p (k w)")).then_inc(stored[q], 16)

        @block.gpsimd
        def _(pool):
            gather_rows(nc, m, pool, idx, g, D + 2, m.table1, s_staged, gathered)

        @block.sync
        def _(sp):
            load_attributes(nc, m, sp, m.ea16, lambda q, k: g[:, q, k, D + 2:L1W], UNITS, s_used, attrs)


def load_attributes(nc, m, sp, source, place, slots, s_used, came):
    with nc.sync.Fori(0, TRIPS) as i:
        for q in range(UNITS):
            n = i * UNITS + q
            _, firsts = nc.values_load_multi_w_load_instructions(
                m.tile_row[0:1, bass.ds(n * UNIT, UNIT)], engines=(mybir.EngineType.SP,), min_val=0,
                max_val=(STEPS - 1) * P,
                skip_runtime_bounds_check_because="it is P times a count of begun tiles, less one")
            sp.wait_ge(s_used, done(n, slots))
            for k in range(UNIT):
                sp.dma_start(place(q, k), source[bass.ds(firsts[k], P), :]).then_inc(came[q % slots], 16)


def layer1_nodes_after(nc, m):
    with ExitStack() as ctx:
        y = ctx.enter_context(nc.sbuf_tensor("l1y", [P, BLOCKS * D], fp32))
        inv = ctx.enter_context(nc.sbuf_tensor("l1inv", [P, BLOCKS], fp32))
        s_v = m.sem("l1n_vec")
        s_v2 = m.sem("l1n_vec2")
        acc = node_view(m.acc)
        with nc.Block() as block:
            @block.vector
            def _(v):
                link = Chain(v, s_v)
                link(nc.vector.tensor_scalar(inv[:, :], acc[:, :, D + 1], 1e-8, None, ALU.add))
                link(nc.vector.reciprocal(inv[:, :], inv[:, :]))
                nc.vector.tensor_tensor(acc[:, :, 0:L1W], acc[:, :, 0:L1W], bc_last(inv[:, :], L1W), ALU.mult)
        project(nc, m, "l1p_", L1W, m.wcat, y)
        with nc.Block() as block:
            @block.vector
            def _(v):
                link = Chain(v, s_v2)
                for _ in range(2):
                    link(nc.vector.tensor_tensor(y[:, :], y[:, :], m.xs[:, :], ALU.add))
        layer_norm(nc, m, "l1ln_", y)


def layer2(nc, m):
    width = D + 1
    with ExitStack() as ctx:
        y = ctx.enter_context(nc.sbuf_tensor("l2y", [P, BLOCKS, width], fp32))
        total = ctx.enter_context(nc.sbuf_tensor("l2total", [P, BLOCKS * D], fp32))
        inv = ctx.enter_context(nc.sbuf_tensor("l2inv", [P, BLOCKS], fp32))
        with nc.Block() as block:
            @block.vector
            def _(v):
                nc.vector.memset(y[:, :, D:width], 1.0)
                nc.vector.tensor_copy(y[:, :, 0:D], node_view(m.xs, D))
        for r in range(ROUNDS):
            store_table(nc, m, f"l2_{r}", y, m.table2[r])
            weighted_sum(nc, m, f"l2_{r}", m.weightS, width, table=m.table2[r])
            m.sem.clear()
            s_v = m.sem(f"l2n_vec{r}")
            acc = node_view(m.acc)
            with nc.Block() as block:
                @block.vector
                def _(v):
                    link = Chain(v, s_v)
                    link(nc.vector.tensor_scalar(inv[:, :], acc[:, :, D], 1e-16, None, ALU.add))
                    link(nc.vector.reciprocal(inv[:, :], inv[:, :]))
                    link(nc.vector.tensor_tensor(y[:, :, 0:D], acc[:, :, 0:D], bc_last(inv[:, :], D), ALU.mult))
                    if r == ROUNDS - 1:
                        nc.vector.tensor_tensor(node_view(total, D), y[:, :, 0:D], node_view(m.xs, D), ALU.add)
        layer_norm(nc, m, "l2ln_", total)


def layer3_nodes_before(nc, m):
    with ExitStack() as ctx:
        sb = lambda name, shape, dt=fp32: ctx.enter_context(nc.sbuf_tensor("l3b" + name, shape, dt))
        w1 = sb("node1", [D, H])
        b1 = sb("b_node1", [H, 1])
        w2 = sb("node2", [H, H])
        e1 = sb("edge1", [D, H])
        e1pad = sb("edge1_padded", [P, H])
        ueT = sb("ueT_padded", [D, P])
        xT = sb("xT", [D, GROUP * P])
        r = sb("relu", [H, GROUP * P])
        part = sb("group", [P, GROUP, P])
        out = sb("rows", [P, GROUP, D + H])
        s_in, s_v, s_w, s_p, s_g, s_t, s_tc, s_h, s_r, s_m, s_o = (
            m.sem("l3b_" + n) for n in
            ("in", "vec", "weights", "product", "group", "turned", "turned_copied", "hidden", "relu",
             "rows_ready", "rows_copied"))
        s_st, s_free = m.sem("l3b_stored"), m.sem("l3b_out_free")
        halves = ((0, 4), (4, GROUP))
        block = ctx.enter_context(nc.Block())

        @block.sync
        def _(sp):
            sp.dma_start(w1[:, :], m.L3_gnn_W_node1).then_inc(s_in, 16)
            sp.dma_start(b1[:, :], m.L3_gnn_b_node1.rearrange("(d o) -> d o", o=1)).then_inc(s_in, 16)
            sp.dma_start(w2[:, :], m.L3_gnn_W_node2).then_inc(s_in, 16)
            sp.dma_start(e1[:, :], m.L3_gnn_W_edge1).then_inc(s_in, 16)
            sp.dma_start(m.be1[:, :], m.L3_gnn_b_edge1.rearrange("(d o) -> d o", o=1)).then_inc(s_in, 16)
            sp.dma_start(m.we2[:, :], m.L3_gnn_W_edge2).then_inc(s_in, 16)
            sp.dma_start(m.wcomb[:, :], m.L3_gnn_W_comb).then_inc(s_in, 16)
            sp.wait_ge(s_w, 2)
            sp.dma_start(e1pad[0:D, :], m.L3_gnn_W_edge1).then_inc(s_in, 16)
            sp.dma_start(ueT[:, D:P], m.ueT).then_inc(s_in, 16)
            sp.sem_inc(s_free, CREDIT)
            with nc.sync.Fori(0, BLOCKS // GROUP) as i:
                sp.wait_ge(s_o, done(i))
                sp.dma_start(m.table3[bass.ds(i * GROUP * P, GROUP * P), :].rearrange("(b p) w -> p b w", p=P),
                             out[:, :, :]).then_inc(s_st, 16)
                sp.wait_ge(s_st, 16 * i + 16)
                sp.sem_inc(s_free, 1)

        @block.vector
        def _(v):
            nc.vector.memset(e1pad[:, :], 0.0).then_inc(s_w, 1)
            nc.vector.memset(ueT[:, :], 0.0).then_inc(s_w, 1)
            nc.vector.memset(part[:, :, :], 0.0).then_inc(s_w, 1)
            nc.vector.tensor_copy(node_view(m.xb)[:, :, 0:D], node_view(m.xs, D))
            v.wait_ge(s_in, 16 * 9)
            v.wait_ge(s_p, 1)
            nc.vector.tensor_scalar(m.wmix[:, :], m.ps[1][3][:, 0:H], 0.2, None, ALU.mult).then_inc(s_v, 1)
            v.wait_ge(s_v, 1)
            nc.vector.scalar_tensor_tensor(m.wmix[:, :], e1pad[:, :], 0.8, m.wmix[:, :], ALU.mult, ALU.add)
            v.sem_inc(s_tc, CREDIT)
            v.sem_inc(s_o, CREDIT)
            with nc.vector.Fori(0, BLOCKS // GROUP) as i:
                v.wait_ge(s_t, done(i))
                nc.vector.tensor_copy(xT[:, 0:4 * P], m.ps[0][0][0:D, :])
                nc.vector.tensor_copy(xT[:, 4 * P:GROUP * P], m.ps[0][1][0:D, 0:3 * P]).then_inc(s_tc, 1)
                v.wait_ge(s_m, done(i))
                v.wait_ge(s_free, done(i, 1))
                v.wait_ge(s_g, done(i))
                nc.vector.tensor_copy(out[:, :, 0:D], part[:, :, 0:D])
                nc.vector.tensor_copy(out[:, 0:4, D:D + H], m.ps[1][0][:, :].rearrange("p (b d) -> p b d", d=H))
                nc.vector.tensor_copy(out[:, 4:GROUP, D:D + H],
                                      m.ps[1][1][:, 0:3 * P].rearrange("p (b d) -> p b d", d=H)).then_inc(s_o, 1)

        @block.tensor
        def _(pe):
            for s in (s_t, s_h, s_m):
                pe.sem_inc(s, CREDIT)
            pe.wait_ge(s_in, 16 * 9)
            nc.tensor.matmul(m.ps[1][3][:, 0:H], ueT[:, :], e1[:, :], start=True, stop=True).then_inc(s_p, 1)
            with nc.tensor.Fori(0, BLOCKS // GROUP) as i:
                pe.wait_ge(s_g, done(i))
                pe.wait_ge(s_tc, done(i, 1))
                for k in range(GROUP):
                    last = nc.tensor.transpose(m.ps[0][k // 4][:, k % 4 * P:(k % 4 + 1) * P],
                                               part[:, k, :], m.ident[:, :])
                last.then_inc(s_t, 1)
                pe.wait_ge(s_tc, done(i))
                pe.wait_ge(s_r, done(i, 1))
                for c, (lo, hi) in enumerate(halves):
                    last = nc.tensor.matmul(m.ps[0][2 + c][:, 0:(hi - lo) * P], w1[:, :],
                                            xT[:, lo * P:hi * P], start=True, stop=True)
                last.then_inc(s_h, 1)
                pe.wait_ge(s_r, done(i))
                pe.wait_ge(s_o, done(i, 1))
                for k in range(GROUP):
                    last = nc.tensor.matmul(m.ps[1][k // 4][:, k % 4 * H:(k % 4 + 1) * H],
                                            r[:, k * P:(k + 1) * P], w2[:, :], start=True, stop=True)
                last.then_inc(s_m, 1)

        @block.scalar
        def _(act):
            act.sem_inc(s_g, CREDIT)
            act.sem_inc(s_r, CREDIT)
            act.wait_ge(s_in, 16 * 9)
            act.wait_ge(s_w, 3)
            with nc.scalar.Fori(0, BLOCKS // GROUP) as i:
                act.wait_ge(s_o, done(i, 1))
                nc.scalar.copy(part[:, :, 0:D], m.xs[:, bass.ds(i * GROUP * D, GROUP * D)].rearrange(
                    "p (b d) -> p b d", d=D)).then_inc(s_g, 1)
                act.wait_ge(s_h, done(i))
                for c, (lo, hi) in enumerate(halves):
                    last = nc.scalar.activation(r[:, lo * P:hi * P], m.ps[0][2 + c][:, 0:(hi - lo) * P],
                                                ACT.Relu, bias=b1[:, 0:1])
                last.then_inc(s_r, 1)


def layer3_edges(nc, m):
    with ExitStack() as ctx:
        sb = lambda name, shape, dt=fp32: ctx.enter_context(nc.sbuf_tensor("l3" + name, shape, dt))
        W3 = D + H
        SLOTS = 4
        g = sb("rows", [P, UNITS, UNIT, W3])
        idx = sb("idx", [P, UNITS, UNIT], i32)
        col = sb("columns", [P, UNITS, 1, UNIT])
        pre = sb("pre", [P, SLOTS, UNIT, P])
        oh = sb("onehot", [P, 2, UNIT, P])
        ohT = sb("onehotT", [P, 2, UNIT * P])
        preT = sb("preT", [P, 2, UNIT * P])
        r = sb("relu", [P, 2, UNIT * P])
        both = sb("both", [P, 2, UNIT, H])
        bothT = sb("bothT", [P, 2, UNIT * P])
        val = sb("values", [P, 2, UNIT * D])
        gathered = [m.sem(f"l3gathered{q}") for q in range(UNITS)]
        attrs = [m.sem(f"l3attrs{q}") for q in range(SLOTS)]
        (s_staged, s_oh, s_t, s_tc, s_hd, s_pre, s_pt, s_ptc, s_mix, s_r, s_m2, s_both, s_bt, s_btc, s_comb,
         s_val, s_sum, s_add) = (m.sem("l3" + n) for n in
                                 ("staged", "onehot_ready", "onehot_turned", "onehotT_copied", "dst_rows",
                                  "pre_ready", "pre_turned", "preT_copied", "mixed", "relu_ready", "m2_ready",
                                  "both_ready", "both_turned", "bothT_copied", "combined", "values_ready",
                                  "summed", "added"))
        pairs = lambda i: [[(q0 + u, u, i * UNITS + (q0 + u)) for u in range(2)] for q0 in range(0, UNITS, 2)]
        block = ctx.enter_context(nc.Block())

        @block.vector
        def _(v):
            for s in (s_oh, s_pre, s_ptc, s_both):
                v.sem_inc(s, CREDIT)
            begin_sums(nc, m, v, s_add)
            with nc.vector.Fori(0, TRIPS) as i:
                for pair in pairs(i):
                    for q, u, n in pair:
                        v.wait_ge(s_staged, done(n))
                        v.wait_ge(s_sum, done(n, 2))
                        for k in range(UNIT):
                            last = nc.vector.tensor_scalar(oh[:, u, k, :], m.iota[:, :],
                                                           col[:, q, 0, k:k + 1], None, ALU.is_equal)
                        last.then_inc(s_oh, 1)
                    for q, u, n in pair:
                        add_sums(nc, m, v, n * UNIT, m.ps[u][3], D, s_add)
                    for q, u, n in pair:
                        v.wait_ge(s_hd, done(n))
                        v.wait_ge(gathered[q], 16 * UNIT * i + 16 * UNIT)
                        nc.vector.tensor_tensor(pre[:, q % SLOTS, :, D:P], g[:, q, :, 0:D],
                                                m.ps[u][1][:, 0:UNIT * D].rearrange("p (k d) -> p k d", d=D),
                                                ALU.mult).then_inc(s_pre, 1)
                    for q, u, n in pair:
                        v.wait_ge(s_pt, done(n))
                        nc.vector.tensor_copy(preT[:, u, :], m.ps[u][2][:, :]).then_inc(s_ptc, 1)
                    for q, u, n in pair:
                        v.wait_ge(s_m2, done(n))
                        nc.vector.tensor_tensor(both[:, u, :, :], g[:, q, :, D:W3],
                                                m.ps[u][0][:, :].rearrange("p (k d) -> p k d", d=H),
                                                ALU.mult).then_inc(s_both, 1)
            for n in (TRIPS * UNITS, TRIPS * UNITS + 1):
                v.wait_ge(s_sum, done(n, 2))
                add_sums(nc, m, v, n * UNIT, m.ps[n % 2][3], D, s_add)

        @block.tensor
        def _(pe):
            for s in (s_t, s_hd, s_pt, s_mix, s_m2, s_bt, s_comb, s_sum):
                pe.sem_inc(s, CREDIT)
            with nc.tensor.Fori(0, TRIPS) as i:
                for pair in pairs(i):
                    for q, u, n in pair:
                        pe.wait_ge(s_oh, done(n))
                        for k in range(UNIT):
                            last = nc.tensor.transpose(m.ps[u][0][:, k * P:(k + 1) * P], oh[:, u, k, :],
                                                       m.ident[:, :])
                        last.then_inc(s_t, 1)
                    for q, u, n in pair:
                        pe.wait_ge(s_tc, done(n))
                        offsets = block_offsets(nc, m, (n + 2) * UNIT, mybir.EngineType.PE)
                        for k in range(UNIT):
                            last = nc.tensor.matmul(m.ps[u][1][:, k * D:(k + 1) * D], ohT[:, u, k * P:(k + 1) * P],
                                                    m.xb[:, bass.ds(offsets[k], D)], start=True, stop=True)
                        last.then_inc(s_hd, 1)
                    for q, u, n in pair:
                        pe.wait_ge(s_pre, done(n))
                        pe.wait_ge(attrs[q % SLOTS], 16 * UNIT * (UNITS // SLOTS) * i + 16 * UNIT * (q // SLOTS + 1))
                        for k in range(UNIT):
                            last = nc.tensor.transpose(m.ps[u][2][:, k * P:(k + 1) * P], pre[:, q % SLOTS, k, :],
                                                       m.ident[:, :])
                        last.then_inc(s_pt, 1)
                    for q, u, n in pair:
                        pe.wait_ge(s_ptc, done(n))
                        pe.wait_ge(s_add, added(n))
                        nc.tensor.matmul(m.ps[u][3][:, :], m.wmix[:, :], preT[:, u, :], start=True,
                                         stop=True).then_inc(s_mix, 1)
                    for q, u, n in pair:
                        pe.wait_ge(s_r, done(n))
                        for k in range(UNIT):
                            last = nc.tensor.matmul(m.ps[u][0][:, k * H:(k + 1) * H], r[:, u, k * P:(k + 1) * P],
                                                    m.we2[:, :], start=True, stop=True)
                        last.then_inc(s_m2, 1)
                    for q, u, n in pair:
                        pe.wait_ge(s_both, done(n))
                        for k in range(UNIT):
                            last = nc.tensor.transpose(m.ps[u][2][:, k * P:(k + 1) * P], both[:, u, k, :],
                                                       m.ident[:, :])
                        last.then_inc(s_bt, 1)
                    for q, u, n in pair:
                        pe.wait_ge(s_btc, done(n))
                        for k in range(UNIT):
                            last = nc.tensor.matmul(m.ps[u][1][:, k * D:(k + 1) * D], bothT[:, u, k * P:(k + 1) * P],
                                                    m.wcomb[:, :], start=True, stop=True)
                        last.then_inc(s_comb, 1)
                    for q, u, n in pair:
                        pe.wait_ge(s_val, done(n))
                        for k in range(UNIT):
                            last = nc.tensor.matmul(m.ps[u][3][:, k * D:(k + 1) * D], oh[:, u, k, :],
                                                    val[:, u, k * D:(k + 1) * D], start=True, stop=True)
                        last.then_inc(s_sum, 1)

        @block.scalar
        def _(act):
            for s in (s_tc, s_r, s_btc, s_val):
                act.sem_inc(s, CREDIT)
            stage_first(nc, m, act, idx, col, (m.dstS,), s_staged)
            with nc.scalar.Fori(0, TRIPS) as i:
                for pair in pairs(i):
                    for q, u, n in pair:
                        stage_unit(nc, m, act, n + LEAD, (q + LEAD) % UNITS, idx, col, (m.dstS,), s_sum, s_staged)
                    for q, u, n in pair:
                        act.wait_ge(s_t, done(n))
                        nc.scalar.copy(ohT[:, u, :], m.ps[u][0][:, :]).then_inc(s_tc, 1)
                    for q, u, n in pair:
                        act.wait_ge(s_mix, done(n))
                        nc.scalar.activation(r[:, u, :], m.ps[u][3][:, :], ACT.Relu,
                                             bias=m.be1[:, 0:1]).then_inc(s_r, 1)
                    for q, u, n in pair:
                        act.wait_ge(s_bt, done(n))
                        nc.scalar.copy(bothT[:, u, :], m.ps[u][2][:, :]).then_inc(s_btc, 1)
                    for q, u, n in pair:
                        act.wait_ge(s_comb, done(n))
                        nc.scalar.activation(val[:, u, :], m.ps[u][1][:, 0:UNIT * D], ACT.Tanh).then_inc(s_val, 1)

        @block.gpsimd
        def _(pool):
            gather_rows(nc, m, pool, idx, g, W3, m.table3, s_staged, gathered)

        @block.sync
        def _(sp):
            load_attributes(nc, m, sp, m.ea64, lambda q, k: pre[:, q % SLOTS, k, 0:D], SLOTS, s_sum, attrs)


def layer3_nodes_after(nc, m):
    with ExitStack() as ctx:
        y = ctx.enter_context(nc.sbuf_tensor("l3y", [P, BLOCKS * D], fp32))
        s_v, s_out = m.sem("l3n_vec"), m.sem("l3n_out")
        with nc.Block() as block:
            @block.vector
            def _(v):
                link = Chain(v, s_v)
                link(nc.vector.tensor_tensor(node_view(y, D), node_view(m.acc)[:, :, 0:D], node_view(m.xs, D),
                                             ALU.add))
                link(nc.vector.tensor_tensor(y[:, :], y[:, :], m.xs[:, :], ALU.add))
        layer_norm(nc, m, "l3ln_", y)
        with nc.Block() as block:
            @block.sync
            def _(sp):
                full = N // P
                sp.dma_start(m.out[0:full * P].rearrange("(b p) d -> p b d", p=P),
                             node_view(m.xs, D)[:, 0:full, :]).then_inc(s_out, 16)
                sp.dma_start(m.out[full * P:N], m.xs[0:N - full * P, full * D:(full + 1) * D]).then_inc(s_out, 16)
                sp.wait_ge(s_out, 32)


def build(nc, a):
    ctx = ExitStack()
    with ctx:
        m = Program()
        m.L0_gnn_gamma_gathered_b = a["L0_gnn_gamma_gathered_b"]
        m.L0_gnn_gamma_gathered_w = a["L0_gnn_gamma_gathered_w"]
        m.L0_gnn_gamma_self_w = a["L0_gnn_gamma_self_w"]
        m.L0_gnn_mlp_b1 = a["L0_gnn_mlp_b1"]
        m.L0_gnn_mlp_b2 = a["L0_gnn_mlp_b2"]
        m.L0_gnn_mlp_w1 = a["L0_gnn_mlp_w1"]
        m.L0_gnn_mlp_w2 = a["L0_gnn_mlp_w2"]
        m.L0_gnn_pd_a = a["L0_gnn_pd_a"]
        m.L0_gnn_pd_b = a["L0_gnn_pd_b"]
        m.L1_gnn_We = a["L1_gnn_We"]
        m.L1_gnn_Wn = a["L1_gnn_Wn"]
        m.L1_gnn_att_dst = a["L1_gnn_att_dst"]
        m.L1_gnn_att_edge = a["L1_gnn_att_edge"]
        m.L1_gnn_att_src = a["L1_gnn_att_src"]
        m.L3_gnn_W_comb = a["L3_gnn_W_comb"]
        m.L3_gnn_W_edge1 = a["L3_gnn_W_edge1"]
        m.L3_gnn_W_edge2 = a["L3_gnn_W_edge2"]
        m.L3_gnn_W_node1 = a["L3_gnn_W_node1"]
        m.L3_gnn_W_node2 = a["L3_gnn_W_node2"]
        m.L3_gnn_b_edge1 = a["L3_gnn_b_edge1"]
        m.L3_gnn_b_node1 = a["L3_gnn_b_node1"]
        m.c_bins = a["c_bins"]
        m.c_ident = a["c_ident"]
        m.c_iota = a["c_iota"]
        m.c_step = a["c_step"]
        m.dst_flat = a["dst_flat"]
        m.ea16 = a["ea16"]
        m.ea64 = a["ea64"]
        m.ew = a["ew"]
        m.ew2 = a["ew2"]
        m.out = a["out"]
        m.src = a["src"]
        m.ueT = a["ueT"]
        m.weT = a["weT"]
        m.wnT = a["wnT"]
        m.x = a["x"]
        m.sem = Semaphores(nc)
        sb = lambda name, shape, dt: ctx.enter_context(nc.sbuf_tensor(name, shape, dt))
        dr = lambda name, shape: nc.dram_tensor(name, shape, fp32).ap()
        m.ps = [[ctx.enter_context(nc.psum_tensor(f"ps{u}{x}", [P, 512], fp32)) for x in range(4)]
                for u in range(2)]
        m.ident = sb("ident", [P, P], fp32)
        m.iota = sb("iota", [P, P], fp32)
        m.step_col = sb("step_col", [P, CHUNKS], fp32)
        m.dstS = sb("dst_steps", [P, STEPS + LEAD * UNIT], fp32)
        m.srcS = sb("src_steps", [P, STEPS + LEAD * UNIT], fp32)
        m.ewS = sb("ew_steps", [P, STEPS + LEAD * UNIT], fp32)
        m.ew2S = sb("ew2_steps", [P, STEPS + LEAD * UNIT], fp32)
        m.tile_row = sb("tile_row", [1, STEPS], i32)
        m.off_row = sb("offset_row", [1, 2 * UNIT + STEPS], i32)
        m.d_extra = dr("d_extra", (STEPS,))
        m.d_pos = dr("d_pos", (STEPS,))
        m.d_q = dr("d_q", (STEPS, QW))
        m.d_tb = dr("d_tb", (2, STEPS))
        m.d_start, m.d_end, m.d_ewm, m.d_mine = (dr(name, (STEPS * P,)) for name in
                                                 ("d_start", "d_end", "d_ewm", "d_mine"))
        m.d_ew = dr("d_ew", (1, STEPS * P))
        m.d_score = dr("d_score", (STEPS * P,))
        m.d_weight = dr("d_weight", (STEPS * P,))
        m.d_tail = dr("d_tail", (2, 2, P))
        m.d_carry = dr("d_carry", (2, P))
        m.weightS = sb("weight_steps", [P, STEPS + LEAD * UNIT], fp32)
        m.scoreS = sb("score_steps", [P, STEPS], fp32)
        m.ve = sb("edge_att", [P, ED], fp32)
        m.wcat = sb("wcat", [L1W, D], fp32)
        m.be1 = sb("b_edge1", [H, 1], fp32)
        m.we2 = sb("w_edge2", [H, H], fp32)
        m.wcomb = sb("w_comb", [H, D], fp32)
        m.wmix = sb("w_mix", [P, H], fp32)
        m.table1 = dr("table1", (NPAD, D + 2))
        m.table2 = [dr(f"table2_{r}", (NPAD, D + 1)) for r in range(ROUNDS)]
        m.table3 = dr("table3", (NPAD, D + H))
        m.d_zd = dr("d_zd", (NPAD,))
        m.d_rows = dr("d_rows", (STEPS // UNIT * P, UNIT * L1W))
        m.bins = sb("bins", [P, BINS + 1], fp32)
        m.w1 = sb("w1", [1, D], fp32)
        m.b1 = sb("b1", [D, 1], fp32)
        m.w2b = sb("w2b", [D + 1, BINS], fp32)
        m.gw = sb("gw", [P, D], fp32)
        m.gb = sb("gb", [P, D], fp32)
        m.a, m.b, m.b0, m.na, m.tiny = (sb("pd_" + name, [P, 1], fp32) for name in
                                        ("a", "b", "b0", "na", "tiny"))
        load_edges(nc, m)
        place_steps(nc, m)
        m.acc = sb("acc", [P, BLOCKS * P], fp32)
        m.xb = sb("node_rows", [P, BLOCKS * P], fp32)
        m.xs = sb("node_x", [P, BLOCKS * D], fp32)
        layer0_nodes_before(nc, m)
        layer0_edges(nc, m)
        layer0_nodes_after(nc, m)
        m.sem.clear()
        layer1_nodes_before(nc, m)
        layer1_scores(nc, m)
        m.sem.clear()
        edge_softmax(nc, m, "w1_", m.weightS, score=m.scoreS, floor=-1e9)
        weighted_sum(nc, m, "l1_", m.weightS, L1W, stored=m.d_rows)
        layer1_nodes_after(nc, m)
        m.sem.clear()
        edge_softmax(nc, m, "w2_", m.weightS)
        layer2(nc, m)
        m.sem.clear()
        layer3_nodes_before(nc, m)
        layer3_edges(nc, m)
        layer3_nodes_after(nc, m)


def kernel(**inputs):
    import concourse.bacc as _bacc
    from concourse.bass_utils import run_bass_kernel_spmd as _run

    nc = _bacc.Bacc("TRN2", target_bir_lowering=False, num_devices=1)
    x = {k: np.asarray(v) for k, v in inputs.items()}
    rows = STEPS * P

    def padded(v, fill):
        out = np.full((rows,) + v.shape[1:], fill, v.dtype)
        out[:E] = v
        return out

    dst = np.full(rows + 2, PAD_NODE, np.int32)
    dst[0], dst[-1] = -1, NPAD
    dst[1:E + 1] = x["dst"]
    nodes = np.zeros((NPAD, D), np.float32)
    nodes[:N] = x["x"]
    arrays = {
        "x": nodes,
        "dst_flat": dst,
        "src": padded(x["src"], 0).reshape(STEPS, P),
        "ew": padded(x["edge_weight"], 0).reshape(STEPS, P),
        "ew2": padded(x["edge_weight_n2"], 0).reshape(STEPS, P),
        "ea16": padded(x["edge_attr_16"], 0),
        "ea64": padded(x["edge_attr_64"], 0),
        "c_ident": np.eye(P, dtype=np.float32),
        "c_iota": np.tile(np.arange(P, dtype=np.float32), (P, 1)),
        "c_step": np.ascontiguousarray(np.arange(STEPS, dtype=np.float32).reshape(CHUNKS, P).T),
        "c_bins": np.tile(np.arange(BINS + 1, dtype=np.float32) / BINS, (P, 1)),
        "wnT": np.ascontiguousarray(x["L1_gnn_Wn"].T),
        "ueT": np.ascontiguousarray(x["L3_gnn_W_ue"].T),
        "weT": np.ascontiguousarray(x["L1_gnn_We"].T),
    }
    for k, v in x.items():
        if k.startswith("L"):
            arrays[k] = np.ascontiguousarray(v)
    a = {}
    for k, v in arrays.items():
        a[k] = nc.dram_tensor(k, v.shape, mybir.dt.from_np(v.dtype), kind="ExternalInput").ap()
    a["out"] = nc.dram_tensor("out", (N, D), fp32, kind="ExternalOutput").ap()
    build(nc, a)
    r = _run(nc, [arrays], core_ids=[0])
    return r.results[0]["out"]
```

```python
import numpy as np
from contextlib import ExitStack
import concourse.bass as bass
from concourse import mybir

P = 128
N = 6250
E = 206250
D = 64
H = 128
ED = 16
ROUNDS = 3
BINS = 32
BLOCKS = -(-N // P)
NPAD = BLOCKS * P
TILES = -(-E // P)
UNIT = 4
UNITS = 8
LEAD = 4
ITER = UNIT * UNITS
STEPS = -(-(TILES + BLOCKS - 1) // P) * P
CHUNKS = STEPS // P
TRIPS = STEPS // ITER
ALL_UNITS = TRIPS * UNITS
L0_SLOTS = 8
PAD_NODE = NPAD - 1
CREDIT = UNITS
FAR = -1.5e38
TINY = 2.0 ** -63
QF = 6
QW = QF * P + 2
L1W = D + 2 + ED
GROUP = 7
assert TRIPS * ITER == STEPS and BLOCKS % GROUP == 0 and PAD_NODE >= N

fp32 = mybir.dt.float32
i32 = mybir.dt.int32
bf16 = mybir.dt.bfloat16
ALU = mybir.AluOpType
ACT = mybir.ActivationFunctionType
AX = mybir.AxisListType


class Program:
    pass


class Chain:

    def __init__(self, eng, sem, start=0):
        self.eng, self.sem, self.n = eng, sem, start

    def __call__(self, ins):
        self.n = self.n + 1
        ins.then_inc(self.sem, 1)
        self.eng.wait_ge(self.sem, self.n)


def done(unit, back=0):
    return unit + (CREDIT + 1 - back)


def bc_last(ap, n):
    return ap.unsqueeze(2).to_broadcast([ap.shape[0], ap.shape[1], n])


def bc_mid(ap, n):
    return ap.unsqueeze(1).to_broadcast([ap.shape[0], n, ap.shape[1]])


def load_edges(nc, m):
    with ExitStack() as ctx:
        sb = lambda name, shape, dt: ctx.enter_context(nc.sbuf_tensor(name, shape, dt))
        cur = sb("dst_cur", [P, CHUNKS, P], i32)
        prev = sb("dst_prev", [P, CHUNKS, P], i32)
        nxt = sb("dst_next", [P, CHUNKS, P], i32)
        srci = sb("src_rows", [P, CHUNKS, P], i32)
        q = sb("edge_fields", [P, CHUNKS, QW], fp32)
        first = sb("first_block", [P, CHUNKS], i32)
        last = sb("last_block", [P, CHUNKS], i32)
        lastf = sb("last_block_f", [P, CHUNKS], fp32)
        extra = sb("extra_steps", [P, CHUNKS], fp32)
        extraT = sb("extra_steps_rows", [CHUNKS, P], fp32)
        extra_row = sb("extra_row", [1, STEPS], fp32)
        run = sb("extra_run", [1, STEPS], fp32)
        ones = sb("ones_row", [1, STEPS], fp32)
        pos = sb("pos_row", [1, STEPS], fp32)
        ps = m.ps[0][0]
        s_in, s_w, s_c, s_row, s_v, s_pos, s_posq, s_q, s_t, s_ct = (
            m.sem(n) for n in ("le_dst", "le_weights", "le_const", "le_row", "le_vec",
                                            "le_pos_out", "le_pos_in", "le_table", "le_pe", "le_rows"))
        flat = lambda off: m.dst_flat[off:off + STEPS * P].rearrange("(c p e) -> p c e", p=P, e=P)
        block = ctx.enter_context(nc.Block())

        @block.vector
        def _(v):
            link = Chain(v, s_v)
            v.wait_ge(s_in, 64)
            link(nc.vector.tensor_scalar(first[:, :], cur[:, :, 0], 7, None, ALU.arith_shift_right))
            link(nc.vector.tensor_scalar(last[:, :], cur[:, :, P - 1], 7, None, ALU.arith_shift_right))
            link(nc.vector.tensor_copy(q[:, :, QF * P + 1], first[:, :]))
            link(nc.vector.tensor_copy(lastf[:, :], last[:, :]))
            link(nc.vector.tensor_tensor(extra[:, :], lastf[:, :], q[:, :, QF * P + 1], ALU.subtract))
            v.wait_ge(s_t, 1)
            nc.vector.tensor_copy(extraT[:, :], ps[0:CHUNKS, 0:P]).then_inc(s_ct, 1)
            link(nc.vector.tensor_copy(q[:, :, 0:P], cur[:, :, :]))
            link(nc.vector.tensor_copy(q[:, :, P:2 * P], srci[:, :, :]))
            link(nc.vector.tensor_tensor(q[:, :, 4 * P:5 * P], cur[:, :, :], prev[:, :, :], ALU.not_equal))
            link(nc.vector.tensor_tensor(q[:, :, 5 * P:6 * P], cur[:, :, :], nxt[:, :, :], ALU.not_equal))
            v.wait_ge(s_c, 48)
            v.wait_ge(s_row, 32)
            link(nc.vector.memset(ones[:, :], 1.0))
            link(nc.vector.tensor_tensor_scan(out=run[:, :], data0=extra_row[:, :], data1=ones[:, :],
                                              initial=-1.0, op0=ALU.add, op1=ALU.add))
            nc.vector.tensor_tensor(pos[:, :], run[:, :], extra_row[:, :], ALU.subtract).then_inc(s_pos, 1)
            m.le_vec_n = link.n

        @block.sync
        def _(sp):
            sp.dma_start(cur[:, :, :], flat(1)).then_inc(s_in, 16)
            sp.dma_start(prev[:, :, :], flat(0)).then_inc(s_in, 16)
            sp.dma_start(nxt[:, :, :], flat(2)).then_inc(s_in, 16)
            sp.dma_start(srci[:, :, :], m.src.rearrange("(c p) e -> p c e", p=P)).then_inc(s_in, 16)
            sp.dma_start(q[:, :, 2 * P:3 * P], m.ew.rearrange("(c p) e -> p c e", p=P)).then_inc(s_w, 16)
            sp.dma_start(q[:, :, 3 * P:4 * P], m.ew2.rearrange("(c p) e -> p c e", p=P)).then_inc(s_w, 16)
            sp.dma_start(m.ident[:, :], m.c_ident).then_inc(s_c, 16)
            sp.dma_start(m.iota[:, :], m.c_iota).then_inc(s_c, 16)
            sp.dma_start(m.step_col[:, :], m.c_step).then_inc(s_c, 16)
            sp.wait_ge(s_ct, 1)
            sp.dma_start(m.d_extra.rearrange("(c p) -> c p", p=P), extraT[:, :]).then_inc(s_row, 16)
            sp.wait_ge(s_row, 16)
            sp.dma_start(extra_row[:, :], m.d_extra.rearrange("(a s) -> a s", a=1)).then_inc(s_row, 16)
            sp.wait_ge(s_pos, 1)
            sp.dma_start(m.d_pos.rearrange("(a s) -> a s", a=1), pos[:, :]).then_inc(s_posq, 16)
            sp.wait_ge(s_posq, 16)
            with nc.allow_non_contiguous_dma(reason="one column of the table"):
                sp.dma_start(q[:, :, QF * P:QF * P + 1],
                             m.d_pos.rearrange("(c p a) -> p c a", p=P, a=1)).then_inc(s_posq, 16)
            sp.wait_ge(s_posq, 32)
            sp.wait_ge(s_w, 32)
            sp.wait_ge(s_v, m.le_vec_n)
            sp.dma_start(m.d_q.rearrange("(c p) w -> p c w", p=P), q[:, :, :]).then_inc(s_q, 16)
            sp.wait_ge(s_q, 16)

        @block.tensor
        def _(pe):
            pe.wait_ge(s_c, 48)
            pe.wait_ge(s_v, 5)
            nc.tensor.transpose(ps[0:CHUNKS, 0:P], extra[:, :], m.ident[:, :]).then_inc(s_t, 1)


def place_steps(nc, m):
    with ExitStack() as ctx:
        sb = lambda name, shape, dt: ctx.enter_context(nc.sbuf_tensor(name, shape, dt))
        posb = sb("pos_all", [P, STEPS], fp32)
        junk = sb("junk", [P, STEPS], fp32)
        count = sb("tiles_begun", [P, CHUNKS], fp32)
        tile = sb("tile_of_step", [P, CHUNKS], fp32)
        tile_i = sb("tile_of_step_i", [P, CHUNKS], i32)
        g = sb("step_fields", [P, CHUNKS, QW], fp32)
        blk = sb("block_of_step", [P, CHUNKS], fp32)
        base = sb("base_of_step", [P, CHUNKS], fp32)
        ok = sb("edge_is_mine", [P, CHUNKS, P], fp32)
        low = sb("low_side", [P, CHUNKS, P], fp32)
        local = sb("dst_in_block", [P, CHUNKS, P], bf16)
        rows = sb("tile_block_rows", [CHUNKS, 2, P], fp32)
        rowf = sb("tile_block_row", [1, 2, STEPS], fp32)
        s_b, s_v, s_ti, s_g, s_ps, s_free, s_rows, s_out, s_row = (
            m.sem(n) for n in ("st_pos", "st_vec", "st_tile", "st_rows_in", "st_psum",
                                            "st_copied", "st_rows", "st_out", "st_row"))
        FIELDS = ((0, m.dstS), (1, m.srcS), (2, m.ewS), (3, m.ew2S))
        block = ctx.enter_context(nc.Block())

        @block.vector
        def _(v):
            link = Chain(v, s_v)
            for t in (m.dstS, m.srcS, m.ewS, m.ew2S, m.weightS):
                nc.vector.memset(t[:, STEPS:], 0.0)
            v.wait_ge(s_b, 16)
            for j in range(CHUNKS):
                link(nc.vector.tensor_scalar(junk[:, :], posb[:, :], m.step_col[:, j:j + 1], None,
                                             ALU.is_le, ALU.add, accum_out=count[:, j:j + 1]))
            link(nc.vector.tensor_scalar(tile[:, :], count[:, :], 1.0, None, ALU.subtract))
            nc.vector.tensor_copy(tile_i[:, :], tile[:, :]).then_inc(s_ti, 1)
            v.wait_ge(s_g, 16 * CHUNKS)
            link(nc.vector.tensor_tensor(blk[:, :], m.step_col[:, :], g[:, :, QF * P], ALU.subtract))
            link(nc.vector.tensor_tensor(blk[:, :], blk[:, :], g[:, :, QF * P + 1], ALU.add))
            link(nc.vector.tensor_scalar(base[:, :], blk[:, :], float(P), None, ALU.mult))
            link(nc.vector.tensor_tensor(g[:, :, 0:P], g[:, :, 0:P], bc_last(base[:, :], P), ALU.subtract))
            link(nc.vector.tensor_scalar(blk[:, :], blk[:, :], float(BLOCKS - 1), None, ALU.min))
            m.st_local = link.n
            link(nc.vector.tensor_copy(local[:, :, :], g[:, :, 0:P]))
            link(nc.vector.tensor_scalar(low[:, :, :], g[:, :, 0:P], 0.0, None, ALU.is_ge))
            link(nc.vector.scalar_tensor_tensor(ok[:, :, :], g[:, :, 0:P], float(P), low[:, :, :],
                                                ALU.is_lt, ALU.mult))
            for j in range(CHUNKS):
                for f, dst in FIELDS:
                    n = len(FIELDS) * j + f
                    v.wait_ge(s_ps, n + 1)
                    nc.vector.tensor_copy(dst[:, j * P:(j + 1) * P],
                                          m.ps[f % 2][f // 2][:, 0:P]).then_inc(s_free, 1)
            for a in range(2):
                v.wait_ge(s_ps, len(FIELDS) * CHUNKS + a + 1)
                nc.vector.tensor_copy(rows[:, a, :], m.ps[a][2][0:CHUNKS, 0:P]).then_inc(s_rows, 1)
            for f in (4, 5):
                link(nc.vector.scalar_tensor_tensor(g[:, :, f * P:(f + 1) * P], ok[:, :, :], FAR,
                                                    g[:, :, f * P:(f + 1) * P], ALU.mult, ALU.mult))
            link(nc.vector.tensor_tensor(g[:, :, 0:P], g[:, :, 2 * P:3 * P], ok[:, :, :], ALU.mult))
            link(nc.vector.tensor_scalar(low[:, :, :], ok[:, :, :], 1.0, -FAR, ALU.subtract, ALU.mult))
            link(nc.vector.tensor_tensor(g[:, :, 0:P], g[:, :, 0:P], low[:, :, :], ALU.add))
            m.st_masked = link.n
            v.wait_ge(s_row, 32)
            nc.vector.tensor_scalar(m.tile_row[:, :], rowf[:, 0, :], float(P), None, ALU.mult)
            nc.vector.tensor_scalar(m.off_row[:, :], rowf[:, 1, :], float(P), None, ALU.mult)

        @block.sync
        def _(sp):
            sp.dma_start(posb[:, :], m.d_pos.partition_broadcast(P)).then_inc(s_b, 16)
            sp.wait_ge(s_v, m.st_masked)
            for f, dst in ((4, m.d_start), (5, m.d_end), (0, m.d_ewm), (2, m.d_ew[0])):
                sp.dma_start(dst.rearrange("(c p e) -> p c e", p=P, e=P),
                             g[:, :, f * P:(f + 1) * P]).then_inc(s_out, 16)
            sp.dma_start(m.d_dst[0].rearrange("(c p e) -> p c e", p=P, e=P), local[:, :, :]).then_inc(s_out, 16)
            sp.dma_start(m.d_mine.rearrange("(c p e) -> p c e", p=P, e=P), ok[:, :, :]).then_inc(s_out, 16)
            sp.wait_ge(s_rows, 2)
            sp.dma_start(m.d_tb.rearrange("a (c p) -> c a p", p=P), rows[:, :, :]).then_inc(s_row, 16)
            sp.wait_ge(s_row, 16)
            sp.dma_start(rowf[:, :, :], m.d_tb.rearrange("(o a) s -> o a s", o=1)).then_inc(s_row, 16)
            sp.wait_ge(s_out, 96)

        @block.gpsimd
        def _(pool):
            pool.wait_ge(s_ti, 1)
            for j in range(CHUNKS):
                nc.gpsimd.indirect_dma_start(g[:, j, :], None, m.d_q,
                                             bass.IndirectOffsetOnAxis(ap=tile_i[:, j:j + 1], axis=0)
                                             ).then_inc(s_g, 16)

        @block.tensor
        def _(pe):
            pe.wait_ge(s_v, m.st_local)
            for j in range(CHUNKS):
                for f, dst in FIELDS:
                    n = len(FIELDS) * j + f
                    if j:
                        pe.wait_ge(s_free, n + 1 - len(FIELDS))
                    nc.tensor.transpose(m.ps[f % 2][f // 2][:, 0:P], g[:, j, f * P:(f + 1) * P],
                                        m.ident[:, :]).then_inc(s_ps, 1)
            for a, src in enumerate((tile, blk)):
                nc.tensor.transpose(m.ps[a][2][0:CHUNKS, 0:P], src[:, :], m.ident[:, :]).then_inc(s_ps, 1)


def edge_softmax(nc, m, tag, dest, score=None, floor=None):
    with ExitStack() as ctx:
        sb = lambda name, shape, dt=fp32: ctx.enter_context(nc.sbuf_tensor(tag + name, shape, dt))
        val = sb("val", [P, STEPS])
        fwd = sb("fwd", [P, STEPS])
        both = sb("both", [P, STEPS])
        start = sb("start", [P, STEPS])
        end = sb("end", [P, STEPS])
        mine = sb("mine", [P, STEPS])
        rows = sb("rows", [P, CHUNKS, P])
        tail = [sb(f"tail{i}", [P, 2]) for i in range(2)]
        tail_row = [sb(f"tail_row{i}", [1, 2, P]) for i in range(2)]
        carry_row = [sb(f"carry_row{i}", [1, P + 1]) for i in range(2)]
        carry = [sb(f"carry{i}", [P, 1]) for i in range(2)]
        s_ps, s_free, s_rows, s_val, s_in, s_v, s_t, s_e, s_w, s_r = (
            m.sem(tag + n) for n in ("pe", "copied", "rows_out", "val_in", "marks_in", "vec",
                                                  "carries", "exp", "w_out", "w_rows"))
        run = lambda d: d.rearrange("(p s) -> p s", p=P)
        bank = lambda j: m.ps[j % 2][j // 2 % 4]
        block = ctx.enter_context(nc.Block())
        at = {}

        @block.vector
        def _(v):
            link = Chain(v, s_v)
            n = 0
            if score is not None:
                for j in range(CHUNKS):
                    v.wait_ge(s_ps, j + 1)
                    nc.vector.tensor_copy(rows[:, j, :], bank(j)[:, 0:P]).then_inc(s_free, 1)
            v.wait_ge(s_in, 48)
            v.wait_ge(s_val, 32 if score is not None else 16)
            for i in range(2):
                link(nc.vector.memset(carry_row[i][:, :], FAR))
            if score is not None:
                link(nc.vector.tensor_tensor(val[:, :], val[:, :], mine[:, :], ALU.mult))
                link(nc.vector.tensor_scalar(mine[:, :], mine[:, :], 1.0, -FAR, ALU.subtract, ALU.mult))
                link(nc.vector.tensor_tensor(val[:, :], val[:, :], mine[:, :], ALU.add))
            for i, (marks, src, out) in enumerate(((start, val, fwd), (end, fwd, both))):
                way = slice(None, None, -1 if i else 1)
                scan = lambda first: nc.vector.tensor_tensor_scan(
                    out=out[:, way], data0=marks[:, way], data1=src[:, way], initial=first,
                    op0=ALU.add, op1=ALU.max)
                link(scan(FAR))
                edge = 0 if i else STEPS - 1
                link(nc.vector.tensor_reduce(tail[i][:, 0:1], marks[:, :], AX.X, ALU.min))
                link(nc.vector.tensor_copy(tail[i][:, 1:2], out[:, edge:edge + 1]))
                at["tail", i] = link.n
                v.wait_ge(s_t, 64 * i + 32)
                into = carry_row[i][:, P - 1::-1] if i else carry_row[i][:, 1:P + 1]
                link(nc.vector.tensor_tensor_scan(out=into, data0=tail_row[i][:, 0, way],
                                                  data1=tail_row[i][:, 1, way], initial=FAR,
                                                  op0=ALU.add, op1=ALU.max))
                at["carry", i] = link.n
                v.wait_ge(s_t, 64 * i + 64)
                link(scan(carry[i][:, 0:1]))
            if floor is not None:
                link(nc.vector.tensor_scalar(both[:, :], both[:, :], floor, None, ALU.max))
            link(nc.vector.tensor_tensor(val[:, :], val[:, :], both[:, :], ALU.subtract))
            link(nc.vector.tensor_scalar(val[:, :], val[:, :], -200.0, None, ALU.max))
            at["arg"] = link.n
            base = CHUNKS if score is not None else 0
            for j in range(CHUNKS):
                v.wait_ge(s_ps, base + j + 1)
                nc.vector.tensor_copy(dest[:, j * P:(j + 1) * P], bank(j)[:, 0:P]).then_inc(s_free, 1)

        @block.sync
        def _(sp):
            for t, d in ((start, m.d_start), (end, m.d_end), (mine, m.d_mine)):
                sp.dma_start(t[:, :], run(d)).then_inc(s_in, 16)
            if score is not None:
                sp.wait_ge(s_free, CHUNKS)
                sp.dma_start(m.d_score.rearrange("(c p e) -> p c e", p=P, e=P), rows[:, :, :]).then_inc(s_val, 16)
                sp.wait_ge(s_val, 16)
                sp.dma_start(val[:, :], run(m.d_score)).then_inc(s_val, 16)
            else:
                sp.dma_start(val[:, :], run(m.d_ewm)).then_inc(s_val, 16)
            with nc.allow_non_contiguous_dma(reason="one value per partition"):
                for i in range(2):
                    sp.wait_ge(s_v, at["tail", i])
                    sp.dma_start(m.d_tail[i].rearrange("a (p o) -> p a o", o=1), tail[i][:, :].unsqueeze(2)).then_inc(s_t, 16)
                    sp.wait_ge(s_t, 64 * i + 16)
                    sp.dma_start(tail_row[i][:, :, :], m.d_tail[i:i + 1]).then_inc(s_t, 16)
                    sp.wait_ge(s_v, at["carry", i])
                    sp.dma_start(m.d_carry[i:i + 1], carry_row[i][:, i:P + i]).then_inc(s_t, 16)
                    sp.wait_ge(s_t, 64 * i + 48)
                    sp.dma_start(carry[i][:, :], m.d_carry[i].rearrange("(p o) -> p o", o=1)).then_inc(s_t, 16)
            sp.wait_ge(s_e, 1)
            sp.dma_start(run(m.d_weight), val[:, :]).then_inc(s_w, 16)
            sp.wait_ge(s_w, 16)
            sp.dma_start(rows[:, :, :], m.d_weight.rearrange("(c p e) -> p c e", p=P, e=P)).then_inc(s_r, 16)

        @block.scalar
        def _(act):
            act.wait_ge(s_v, at["arg"])
            nc.scalar.activation(val[:, :], val[:, :], ACT.Exp).then_inc(s_e, 1)

        @block.tensor
        def _(pe):
            if score is not None:
                for j in range(CHUNKS):
                    if j >= 8:
                        pe.wait_ge(s_free, j - 7)
                    nc.tensor.transpose(bank(j)[:, 0:P], score[:, j * P:(j + 1) * P], m.ident[:, :]).then_inc(s_ps, 1)
            base = CHUNKS if score is not None else 0
            pe.wait_ge(s_r, 16)
            if base:
                pe.wait_ge(s_free, base)
            for j in range(CHUNKS):
                if j >= 8:
                    pe.wait_ge(s_free, base + j - 7)
                nc.tensor.transpose(bank(j)[:, 0:P], rows[:, j, :], m.ident[:, :]).then_inc(s_ps, 1)


def store_table(nc, m, tag, tile, table):
    s_out = m.sem(tag + "table_out")
    with nc.Block() as block:
        @block.sync
        def _(sp):
            sp.dma_start(table.rearrange("(b p) w -> p b w", p=P), tile[:, :, :]).then_inc(s_out, 16)
            sp.wait_ge(s_out, 16)


class Semaphores:

    def __init__(self, nc):
        self.nc, self.out = nc, []

    def __call__(self, name):
        self.out.append(self.nc.alloc_semaphore(name))
        return self.out[-1]

    def clear(self):
        self.nc.clear_and_free_semaphores(self.out)
        self.nc.all_engine_barrier()
        self.out = []


class Ticks:

    def __init__(self, sem, trip, per):
        self.sem, self.trip, self.per, self.n = sem, trip, per, 0

    def __call__(self, ins):
        self.n += 1
        ins.then_inc(self.sem, 1)
        return self.trip * self.per + self.n


class Unit:

    def __init__(self, trip, place):
        turn = 0 if place >= 0 else -1
        self.n, self.slot = trip * UNITS + place, place % UNITS
        self.parity, self.turns = place % 2, trip + (turn + 1)
        self.step = self.n * UNIT


def at_stage(trip, place, lag):
    unit = Unit(trip, place - lag)
    if isinstance(trip, int) and not 0 <= unit.n < ALL_UNITS:
        return None
    return unit


def run_trips(eng, trip_body, drain=True):
    trip_body(0)
    with eng.Fori(1, TRIPS) as trip:
        trip_body(trip)
    if drain:
        trip_body(TRIPS)


def block_offsets(nc, m, unit, engine):
    _, regs = nc.values_load_multi_w_load_instructions(
        m.off_row[0:1, bass.ds(unit.step, UNIT)], engines=(engine,), min_val=0, max_val=(BLOCKS - 1) * P,
        skip_runtime_bounds_check_because="place_steps clamps the blocks to those that exist")
    return regs


def build_and_add(nc, m, v, fresh, late, onehot, width, s_sum, s_added, s_oh, own=range(UNIT),
                  accs=None):
    accs = accs or (m.acc,)
    ahead = (len(own) + 1) // 2
    for k in range(UNIT + ahead):
        if fresh and k < len(own):
            ins = onehot(fresh, own[k])
            if k == len(own) - 1:
                ins.then_inc(s_oh, 1)
        if late and k == ahead - 1:
            offsets = block_offsets(nc, m, late, mybir.EngineType.DVE)
            v.wait_ge(s_sum, done(late.n))
        if late and k >= ahead:
            step = k - ahead
            into = accs[step % len(accs)][:, bass.ds(offsets[step], width)]
            before = late.step + (step + 2 - len(accs))
            v.wait_ge(s_added, max(before, 1) if isinstance(before, int) else before)
            nc.vector.tensor_tensor(into, into, m.ps[late.parity][3][:, step * width:(step + 1) * width],
                                    ALU.add).then_inc(s_added, 1)


def wait_added(eng, unit, back, s_added):
    if not isinstance(unit.n, int) or unit.n >= back:
        eng.wait_ge(s_added, unit.n * UNIT + (UNIT + 1 - back * UNIT))


def wait_bank(pe, unit, ahead, s_other, s_own):
    if isinstance(unit.n, int) and unit.n + ahead >= ALL_UNITS:
        pe.wait_ge(s_own, done(unit.n, 2))
    else:
        pe.wait_ge(s_other, done(unit.n + ahead))


def stage_unit(nc, m, act, unit, idx, col, fields, s_free, s_staged):
    act.wait_ge(s_free, done(unit.n, UNITS))
    if idx is not None:
        nc.scalar.copy(idx[:, unit.slot, :], m.srcS[:, bass.ds(unit.step, UNIT)])
    for f, tile in enumerate(fields):
        last = nc.scalar.copy(col[:, unit.slot, f, :], tile[:, bass.ds(unit.step, UNIT)])
    last.then_inc(s_staged, 1)


def stage_first(nc, m, act, idx, col, fields, s_free, s_staged):
    act.sem_inc(s_staged, CREDIT)
    for n in range(LEAD):
        stage_unit(nc, m, act, Unit(0, n), idx, col, fields, s_free, s_staged)


def gather_rows(nc, m, pool, idx, g, cols, table, s_staged, gathered):
    with nc.gpsimd.Fori(0, TRIPS) as trip:
        for q in range(UNITS):
            pool.wait_ge(s_staged, done(trip * UNITS + q))
            nc.gpsimd.nop(nofuse=True)
            for k in range(UNIT):
                nc.gpsimd.indirect_dma_start(
                    g[:, q, k, 0:cols], None, table,
                    bass.IndirectOffsetOnAxis(ap=idx[:, q, k:k + 1], axis=0)).then_inc(gathered[q], 16)


def weighted_sum(nc, m, tag, weight, width, table=None, stored=None):
    with ExitStack() as ctx:
        sb = lambda name, shape, dt=fp32: ctx.enter_context(nc.sbuf_tensor(tag + name, shape, dt))
        g = sb("rows", [P, UNITS, UNIT, width])
        idx = sb("idx", [P, UNITS, UNIT], i32) if table is not None else None
        col = sb("columns", [P, UNITS, 2, UNIT])
        oh = sb("onehot", [P, 4, UNIT, P])
        gathered = [m.sem(f"{tag}gathered{q}") for q in range(UNITS)]
        s_staged, s_oh, s_oh2, s_sum, s_add = (m.sem(tag + n) for n in
                                               ("staged", "onehot_ready", "other_onehot_ready", "summed",
                                                "added"))
        mine = range(UNIT) if table is not None else range(UNIT - 1)
        others = range(len(mine), UNIT)
        accs = (m.acc,) if table is not None else (m.acc, m.xb)
        per = 16 * UNIT if table is not None else 16
        fields = (m.dstS, weight)
        block = ctx.enter_context(nc.Block())

        def build(eng, unit, k):
            return eng.tensor_scalar(
                oh[:, unit.slot % 4, k, :], m.iota[:, :], col[:, unit.slot, 0, k:k + 1],
                col[:, unit.slot, 1, k:k + 1], ALU.is_equal, ALU.mult)

        @block.vector
        def _(v):
            def onehot(unit, k):
                return build(nc.vector, unit, k)

            def trip_body(trip):
                for j in range(UNITS):
                    fresh, late = at_stage(trip, j, 0), at_stage(trip, j, 2)
                    if fresh:
                        v.wait_ge(s_staged, done(fresh.n))
                        v.wait_ge(s_sum, done(fresh.n, 4))
                    build_and_add(nc, m, v, fresh, late, onehot, width, s_sum, s_add, s_oh, mine, accs)

            v.sem_inc(s_oh, CREDIT)
            for tile in accs[1:]:
                nc.vector.memset(tile[:, :], 0.0)
            nc.vector.memset(m.acc[:, :], 0.0).then_inc(s_add, 1)
            run_trips(nc.vector, trip_body)
            for tile in accs[1:]:
                v.wait_ge(s_add, STEPS + 1)
                nc.vector.tensor_tensor(m.acc[:, :], m.acc[:, :], tile[:, :], ALU.add)

        @block.tensor
        def _(pe):
            def trip_body(trip):
                for j in range(UNITS):
                    unit = at_stage(trip, j, 0)
                    pe.wait_ge(s_oh, done(unit.n))
                    if others:
                        pe.wait_ge(s_oh2, done(unit.n))
                    pe.wait_ge(gathered[unit.slot], per * unit.turns)
                    wait_added(pe, unit, 2, s_add)
                    for k in range(UNIT):
                        last = nc.tensor.matmul(m.ps[unit.parity][3][:, k * width:(k + 1) * width],
                                                oh[:, unit.slot % 4, k, :], g[:, unit.slot, k, :],
                                                start=True, stop=True)
                    last.then_inc(s_sum, 1)

            pe.sem_inc(s_sum, CREDIT)
            run_trips(nc.tensor, trip_body, drain=False)

        @block.scalar
        def _(act):
            stage_first(nc, m, act, idx, col, fields, s_sum, s_staged)
            with nc.scalar.Fori(0, TRIPS) as trip:
                for j in range(UNITS):
                    stage_unit(nc, m, act, Unit(trip, j + LEAD), idx, col, fields, s_sum, s_staged)

        if table is not None:
            @block.gpsimd
            def _(pool):
                gather_rows(nc, m, pool, idx, g, width, table, s_staged, gathered)
        else:
            @block.gpsimd
            def _(pool):
                pool.sem_inc(s_oh2, CREDIT)
                with nc.gpsimd.Fori(0, TRIPS) as trip:
                    for j in range(UNITS):
                        unit = Unit(trip, j)
                        pool.wait_ge(s_staged, done(unit.n))
                        pool.wait_ge(s_sum, done(unit.n, 4))
                        nc.gpsimd.nop(nofuse=True)
                        for k in others:
                            last = build(nc.gpsimd, unit, k)
                        last.then_inc(s_oh2, 1)

            @block.sync
            def _(sp):
                with nc.sync.Fori(0, TRIPS) as trip:
                    for j in range(UNITS):
                        n = trip * UNITS + j
                        sp.wait_ge(s_sum, done(n, UNITS))
                        sp.dma_start(g[:, j, :, :].rearrange("p k w -> p (k w)"),
                                     stored[bass.ds(n * P, P), :]).then_inc(gathered[j], 16)


def layer0_edges(nc, m):
    with ExitStack() as ctx:
        sb = lambda name, shape, dt=fp32: ctx.enter_context(nc.sbuf_tensor("l0" + name, shape, dt))
        g = sb("rows", [P, UNITS, UNIT, D])
        idx = sb("idx", [P, UNITS, UNIT], i32)
        col = sb("columns", [P, UNITS, 3, UNIT])
        dist = sb("dist", [D, 4, UNIT * P])
        oh = sb("onehot", [P, L0_SLOTS, UNIT, P])
        ohT = sb("onehotT", [P, 2, UNIT * P])
        hid = sb("hidden", [D + 1, 2, UNIT * P])
        diff = sb("diff", [P, 2, UNIT * D])
        size = sb("size", [P, 2, UNIT * D])
        log = sb("log", [P, 2, UNIT * D])
        powr = sb("power", [P, 2, UNIT * D])
        val = sb("values", [P, L0_SLOTS, UNIT, 2 * D])
        gathered = [m.sem(f"l0gathered{q}") for q in range(UNITS)]
        came = [m.sem(f"l0dist{q}") for q in range(4)]
        (s_staged, s_oh, s_t, s_tc, s_hc, s_m, s_mlp, s_hd, s_diff, s_size, s_ln, s_pow, s_keep, s_val, s_sum,
         s_add, s_one, s_ind) = (m.sem("l0" + n) for n in
                          ("staged", "onehot_ready", "onehot_turned", "turned_copied", "hidden_ready",
                           "mlp_ready", "mlp_copied", "dst_rows_ready", "diff_ready", "size_ready",
                           "log_ready", "power_ready", "power_kept", "values_ready", "summed", "added",
                           "ones", "indicators_ready"))
        fields = (m.dstS, m.binS, m.ew2S)
        block = ctx.enter_context(nc.Block())

        @block.vector
        def _(v):
            def onehot(unit, k):
                return nc.vector.tensor_scalar(oh[:, unit.slot % L0_SLOTS, k, :], m.iota[:, :],
                                               col[:, unit.slot, 0, k:k + 1], None, ALU.is_equal)

            def indicators(unit):
                nc.vector.tensor_tensor(val[:, unit.slot % L0_SLOTS, :, 0:BINS], bc_mid(m.iota[:, 0:BINS], UNIT),
                                        bc_last(col[:, unit.slot, 1, :], BINS), ALU.is_equal
                                        ).then_inc(s_ind, 1)

            def differences(unit):
                v.wait_ge(s_hd, done(unit.n))
                v.wait_ge(gathered[unit.slot], 16 * UNIT * unit.turns)
                nc.vector.scalar_tensor_tensor(
                    diff[:, unit.parity, :], g[:, unit.slot, :, :].rearrange("p k w -> p (k w)"),
                    m.na[:, 0:1], m.ps[unit.parity][2][:, 0:UNIT * D], ALU.mult, ALU.add).then_inc(s_diff, 1)

            def sizes(unit):
                v.wait_ge(s_diff, done(unit.n))
                nc.vector.scalar_tensor_tensor(size[:, unit.parity, :], diff[:, unit.parity, :], -1.0,
                                               diff[:, unit.parity, :], ALU.mult, ALU.max).then_inc(s_size, 1)

            def keep_powers(unit):
                v.wait_ge(s_pow, done(unit.n))
                nc.vector.scalar_tensor_tensor(powr[:, unit.parity, :], size[:, unit.parity, :], m.low[:, 0:1],
                                               powr[:, unit.parity, :], ALU.is_gt, ALU.mult).then_inc(s_keep, 1)

            def values(unit):
                v.wait_ge(s_keep, done(unit.n))
                v.wait_ge(s_ind, done(unit.n))
                v.wait_ge(s_mlp, done(unit.n))
                for k in range(UNIT):
                    last = nc.vector.scalar_tensor_tensor(
                        val[:, unit.slot % L0_SLOTS, k, D:2 * D], powr[:, unit.parity, k * D:(k + 1) * D],
                        col[:, unit.slot, 2, k:k + 1], val[:, unit.slot % L0_SLOTS, k, 0:D], ALU.mult, ALU.mult)
                last.then_inc(s_val, 1)

            def trip_body(trip):
                for j in range(UNITS):
                    fresh, late = at_stage(trip, j, 0), at_stage(trip, j, 4)
                    if fresh:
                        v.wait_ge(s_staged, done(fresh.n))
                        v.wait_ge(s_sum, done(fresh.n, L0_SLOTS))
                    build_and_add(nc, m, v, fresh, late, onehot, 2 * D, s_sum, s_add, s_oh)
                    for lag, stage in ((2, keep_powers), (1, differences), (0, indicators), (2, values),
                                       (1, sizes)):
                        unit = at_stage(trip, j, lag)
                        if unit:
                            stage(unit)

            nc.vector.memset(hid[D:D + 1, :, :], 1.0).then_inc(s_one, 1)
            for s in (s_oh, s_ind, s_diff, s_size, s_keep, s_val):
                v.sem_inc(s, CREDIT)
            nc.vector.memset(m.acc[:, :], 0.0).then_inc(s_add, 1)
            run_trips(nc.vector, trip_body)

        @block.tensor
        def _(pe):
            def turn_onehots(unit):
                pe.wait_ge(s_oh, done(unit.n))
                pe.wait_ge(s_tc, done(unit.n, 2))
                for k in range(UNIT):
                    last = nc.tensor.transpose(m.ps[unit.parity][0][:, k * P:(k + 1) * P],
                                               oh[:, unit.slot % L0_SLOTS, k, :], m.ident[:, :])
                last.then_inc(s_t, 1)

            def mlp(unit):
                pe.wait_ge(s_hc, done(unit.n))
                pe.wait_ge(s_mlp, done(unit.n, 2))
                for k in range(UNIT):
                    last = nc.tensor.matmul(m.ps[unit.parity][1][:, k * BINS:(k + 1) * BINS],
                                            hid[:, unit.parity, k * P:(k + 1) * P], m.w2b[:, :],
                                            start=True, stop=True)
                last.then_inc(s_m, 1)

            def dst_rows(unit):
                offsets = block_offsets(nc, m, unit, mybir.EngineType.PE)
                pe.wait_ge(s_tc, done(unit.n))
                pe.wait_ge(s_diff, done(unit.n, 2))
                for k in range(UNIT):
                    last = nc.tensor.matmul(m.ps[unit.parity][2][:, k * D:(k + 1) * D],
                                            ohT[:, unit.parity, k * P:(k + 1) * P],
                                            m.xb[:, bass.ds(offsets[k], D)], start=True, stop=True)
                last.then_inc(s_hd, 1)

            def sums(unit):
                pe.wait_ge(s_val, done(unit.n))
                wait_added(pe, unit, 2, s_add)
                for k in range(UNIT):
                    last = nc.tensor.matmul(m.ps[unit.parity][3][:, k * 2 * D:(k + 1) * 2 * D],
                                            oh[:, unit.slot % L0_SLOTS, k, :], val[:, unit.slot % L0_SLOTS, k, :],
                                            start=True, stop=True)
                last.then_inc(s_sum, 1)

            def trip_body(trip):
                for j in range(UNITS):
                    for lag, stage in ((1, dst_rows), (3, sums), (0, turn_onehots), (0, mlp)):
                        unit = at_stage(trip, j, lag)
                        if unit:
                            stage(unit)

            for s in (s_t, s_m, s_hd, s_sum):
                pe.sem_inc(s, CREDIT)
            pe.wait_ge(s_one, 1)
            run_trips(nc.tensor, trip_body)

        @block.scalar
        def _(act):
            def hidden(unit):
                act.wait_ge(came[unit.slot % 4], (unit.turns * 2 - (1 if unit.slot < 4 else 0)) * 16)
                act.wait_ge(s_m, done(unit.n, 2))
                nc.scalar.activation(hid[0:D, unit.parity, :], dist[:, unit.slot % 4, :], ACT.Relu,
                                     bias=m.b1[:, 0:1], scale=m.w1[:, 0:1]).then_inc(s_hc, 1)

            def copy_turned(unit):
                act.wait_ge(s_t, done(unit.n))
                act.wait_ge(s_hd, done(unit.n, 2))
                nc.scalar.copy(ohT[:, unit.parity, :], m.ps[unit.parity][0][:, :]).then_inc(s_tc, 1)

            def mlp_out(unit):
                act.wait_ge(s_m, done(unit.n))
                act.wait_ge(s_sum, done(unit.n, L0_SLOTS))
                nc.scalar.activation(
                    val[:, unit.slot % L0_SLOTS, :, BINS:D],
                    m.ps[unit.parity][1][:, 0:UNIT * BINS].rearrange("p (k w) -> p k w", w=BINS),
                    ACT.Relu).then_inc(s_mlp, 1)

            def logs(unit):
                act.wait_ge(s_size, done(unit.n))
                nc.scalar.activation(log[:, unit.parity, :], size[:, unit.parity, :], ACT.Ln,
                                     bias=m.tiny[:, 0:1]).then_inc(s_ln, 1)

            def powers(unit):
                act.wait_ge(s_ln, done(unit.n))
                act.wait_ge(s_val, done(unit.n, 2))
                nc.scalar.activation(powr[:, unit.parity, :], log[:, unit.parity, :], ACT.Exp,
                                     scale=m.b[:, 0:1]).then_inc(s_pow, 1)

            def trip_body(trip):
                for j in range(UNITS):
                    for lag, stage in ((2, logs),
                                       (-LEAD, lambda unit: stage_unit(nc, m, act, unit, idx, col, fields, s_sum,
                                                                       s_staged)),
                                       (2, powers), (0, hidden), (1, mlp_out), (0, copy_turned)):
                        unit = at_stage(trip, j, lag)
                        if unit:
                            stage(unit)

            nc.scalar.preload_act_table_set("natural_log_exp_and_others")
            for s in (s_tc, s_hc, s_mlp, s_ln, s_pow):
                act.sem_inc(s, CREDIT)
            stage_first(nc, m, act, idx, col, fields, s_sum, s_staged)
            run_trips(nc.scalar, trip_body)

        @block.gpsimd
        def _(pool):
            gather_rows(nc, m, pool, idx, g, D, m.x, s_staged, gathered)

        @block.sync
        def _(sp):
            with nc.sync.Fori(0, TRIPS) as trip:
                for j in range(UNITS):
                    n = trip * UNITS + j
                    sp.wait_ge(s_hc, done(n, 4))
                    sp.dma_start(dist[:, j % 4, :],
                                 m.d_ew[:, bass.ds(n * UNIT * P, UNIT * P)].to_broadcast([D, UNIT * P])
                                 ).then_inc(came[j % 4], 16)


def project(nc, m, tag, width, w, out):
    with ExitStack() as ctx:
        sb = lambda name, shape, dt=fp32: ctx.enter_context(nc.sbuf_tensor(tag + name, shape, dt))
        part = sb("group", [P, GROUP * P])
        turned = sb("group_turned", [P, GROUP * P])
        s_in, s_t, s_tc, s_p, s_out = (m.sem(tag + n) for n in
                                       ("in", "turned", "turned_copied", "product", "out"))
        cut = ((0, 4), (4, GROUP))
        block = ctx.enter_context(nc.Block())

        @block.scalar
        def _(act):
            act.sem_inc(s_in, CREDIT)
            act.sem_inc(s_tc, CREDIT)
            with nc.scalar.Fori(0, BLOCKS // GROUP) as i:
                act.wait_ge(s_t, done(i, 1))
                nc.scalar.copy(part[:, :], m.acc[:, bass.ds(i * GROUP * P, GROUP * P)]).then_inc(s_in, 1)
                act.wait_ge(s_t, done(i))
                act.wait_ge(s_p, done(i, 1))
                nc.scalar.copy(turned[0:width, 0:4 * P], m.ps[0][0][0:width, :])
                nc.scalar.copy(turned[0:width, 4 * P:GROUP * P],
                               m.ps[0][1][0:width, 0:(GROUP - 4) * P]).then_inc(s_tc, 1)

        @block.tensor
        def _(pe):
            pe.sem_inc(s_t, CREDIT)
            pe.sem_inc(s_p, CREDIT)
            with nc.tensor.Fori(0, BLOCKS // GROUP) as i:
                pe.wait_ge(s_in, done(i))
                pe.wait_ge(s_tc, done(i, 1))
                for k in range(GROUP):
                    last = nc.tensor.transpose(m.ps[0][k // 4][0:width, k % 4 * P:(k % 4 + 1) * P],
                                               part[:, k * P:k * P + width], m.ident[:, :])
                last.then_inc(s_t, 1)
                pe.wait_ge(s_tc, done(i))
                pe.wait_ge(s_out, done(i, 1))
                for k in range(GROUP):
                    last = nc.tensor.matmul(m.ps[1][0][:, k * D:(k + 1) * D],
                                            turned[0:width, k * P:(k + 1) * P], w[0:width, :],
                                            start=True, stop=True)
                last.then_inc(s_p, 1)

        @block.vector
        def _(v):
            v.sem_inc(s_out, CREDIT)
            with nc.vector.Fori(0, BLOCKS // GROUP) as i:
                v.wait_ge(s_p, done(i))
                nc.vector.tensor_copy(out[:, bass.ds(i * GROUP * D, GROUP * D)],
                                      m.ps[1][0][:, 0:GROUP * D]).then_inc(s_out, 1)


def layer_norm(nc, m, tag, y):
    with ExitStack() as ctx:
        sb = lambda name, shape, dt=fp32: ctx.enter_context(nc.sbuf_tensor(tag + name, shape, dt))
        mean = sb("mean", [P, BLOCKS])
        sq = sb("squares", [P, BLOCKS * D])
        var = sb("var", [P, BLOCKS])
        dev = sb("dev", [P, BLOCKS])
        s_v, s_d = (m.sem(tag + n) for n in ("vec", "dev"))
        wide = lambda t: t[:, :].rearrange("p (b d) -> p b d", d=D)
        block = ctx.enter_context(nc.Block())

        @block.vector
        def _(v):
            link = Chain(v, s_v)
            link(nc.vector.tensor_reduce(mean[:, :], wide(y), AX.X, ALU.add))
            link(nc.vector.tensor_scalar(mean[:, :], mean[:, :], 1.0 / D, None, ALU.mult))
            link(nc.vector.tensor_tensor(wide(y), wide(y), bc_last(mean[:, :], D), ALU.subtract))
            link(nc.vector.tensor_tensor(sq[:, :], y[:, :], y[:, :], ALU.mult))
            link(nc.vector.tensor_reduce(var[:, :], wide(sq), AX.X, ALU.add))
            link(nc.vector.tensor_scalar(var[:, :], var[:, :], 1.0 / D, 1e-5, ALU.mult, ALU.add))
            m.ln_n = link.n
            v.wait_ge(s_d, 1)
            link(nc.vector.reciprocal(dev[:, :], dev[:, :]))
            nc.vector.tensor_tensor(wide(m.xs), wide(y), bc_last(dev[:, :], D), ALU.mult)

        @block.scalar
        def _(act):
            act.wait_ge(s_v, m.ln_n)
            nc.scalar.activation(dev[:, :], var[:, :], ACT.Sqrt).then_inc(s_d, 1)


def node_view(tile, width=P):
    return tile[:, :].rearrange("p (b w) -> p b w", w=width)


def layer0_nodes_before(nc, m):
    s_in, s_v, s_z = (m.sem(n) for n in ("l0w_in", "l0w_vec", "l0w_zero"))
    block_ctx = ExitStack()
    with block_ctx:
        raw = block_ctx.enter_context(nc.sbuf_tensor("l0w_ab", [P, 2], fp32))
        scaled, whole, flag = (block_ctx.enter_context(nc.sbuf_tensor("l0w_" + n, [P, STEPS], fp32))
                               for n in ("scaled", "whole", "flag"))
        whole_i = block_ctx.enter_context(nc.sbuf_tensor("l0w_whole_i", [P, STEPS], i32))
        block = block_ctx.enter_context(nc.Block())

        @block.sync
        def _(sp):
            sp.dma_start(node_view(m.xs, D), m.x.rearrange("(b p) d -> p b d", p=P)).then_inc(s_in, 16)
            sp.dma_start(m.w1[:, :], m.L0_gnn_mlp_w1.rearrange("o d -> d o")).then_inc(s_in, 16)
            sp.dma_start(m.b1[:, :], m.L0_gnn_mlp_b1.rearrange("(d o) -> d o", o=1)).then_inc(s_in, 16)
            sp.dma_start(m.w2b[0:D, :], m.L0_gnn_mlp_w2).then_inc(s_in, 16)
            sp.dma_start(m.w2b[D:D + 1, :], m.L0_gnn_mlp_b2.rearrange("(o d) -> o d", o=1)).then_inc(s_in, 16)
            sp.dma_start(raw[:, 0:1], m.L0_gnn_pd_a.partition_broadcast(P)).then_inc(s_in, 16)
            sp.dma_start(raw[:, 1:2], m.L0_gnn_pd_b.partition_broadcast(P)).then_inc(s_in, 16)
            sp.dma_start(m.gw[0:D, :], m.L0_gnn_gamma_self_w).then_inc(s_in, 16)
            sp.dma_start(m.gw[D:P, :], m.L0_gnn_gamma_gathered_w).then_inc(s_in, 16)
            sp.dma_start(m.gb[:, :], m.L0_gnn_gamma_gathered_b.partition_broadcast(P)).then_inc(s_in, 16)

        @block.vector
        def _(v):
            link = Chain(v, s_v)
            nc.vector.memset(m.wcat[:, :], 0.0)
            nc.vector.memset(m.binS[:, STEPS:], 0.0)
            link(nc.vector.tensor_scalar(scaled[:, :], m.ewS[:, 0:STEPS], float(BINS), 2.0 * BINS, ALU.mult,
                                         ALU.min))
            link(nc.vector.tensor_scalar(scaled[:, :], scaled[:, :], -2.0 * BINS, None, ALU.max))
            link(nc.vector.tensor_copy(whole_i[:, :], scaled[:, :]))
            link(nc.vector.tensor_copy(whole[:, :], whole_i[:, :]))
            link(nc.vector.tensor_tensor(flag[:, :], whole[:, :], scaled[:, :], ALU.is_gt))
            link(nc.vector.tensor_tensor(whole[:, :], whole[:, :], flag[:, :], ALU.subtract))
            link(nc.vector.tensor_tensor(flag[:, :], whole[:, :], scaled[:, :], ALU.is_equal))
            link(nc.vector.scalar_tensor_tensor(flag[:, :], whole[:, :], 1.0, flag[:, :], ALU.add, ALU.mult))
            link(nc.vector.tensor_tensor(m.binS[:, 0:STEPS], whole[:, :], flag[:, :], ALU.subtract))
            v.wait_ge(s_in, 160)
            link(nc.vector.tensor_scalar(m.a[:, :], raw[:, 0:1], 0.0, 1.0, ALU.max, ALU.min))
            link(nc.vector.scalar_tensor_tensor(m.b[:, :], raw[:, 1:2], -1.0, raw[:, 1:2], ALU.mult, ALU.max))
            nc.vector.memset(m.tiny[:, :], TINY)
            link(nc.vector.tensor_scalar(m.low[:, :], m.b[:, :], 0.0, -1.0, ALU.is_equal, ALU.mult))
            link(nc.vector.tensor_scalar(m.na[:, :], m.a[:, :], 1.0, None, ALU.subtract))
            link(nc.vector.tensor_scalar(node_view(m.xb)[:, :, 0:D], node_view(m.xs, D), m.a[:, 0:1], None,
                                         ALU.mult))


def layer0_nodes_after(nc, m):
    with ExitStack() as ctx:
        y = ctx.enter_context(nc.sbuf_tensor("l0y", [P, BLOCKS * D], fp32))
        inv = ctx.enter_context(nc.sbuf_tensor("l0inv", [P, BLOCKS * D], fp32))
        s_v = m.sem("l0n_vec")
        s_v2 = m.sem("l0n_vec2")
        acc = node_view(m.acc)
        with nc.Block() as block:
            @block.vector
            def _(v):
                link = Chain(v, s_v)
                link(nc.vector.tensor_scalar(node_view(inv, D), acc[:, :, 0:D], 1e-5, None, ALU.add))
                link(nc.vector.reciprocal(inv[:, :], inv[:, :]))
                link(nc.vector.tensor_tensor(acc[:, :, D:P], acc[:, :, D:P], node_view(inv, D), ALU.mult))
                link(nc.vector.tensor_copy(acc[:, :, 0:D], node_view(m.xs, D)))
        project(nc, m, "l0p_", P, m.gw, y)
        with nc.Block() as block:
            @block.vector
            def _(v):
                link = Chain(v, s_v2)
                link(nc.vector.tensor_tensor(node_view(y, D), node_view(y, D), bc_mid(m.gb[:, :], BLOCKS),
                                             ALU.add))
                link(nc.vector.scalar_tensor_tensor(y[:, :], y[:, :], 0.0, m.xs[:, :], ALU.max, ALU.add))
        layer_norm(nc, m, "l0ln_", y)


def layer1_nodes_before(nc, m):
    with ExitStack() as ctx:
        sb = lambda name, shape, dt=fp32: ctx.enter_context(nc.sbuf_tensor("l1b" + name, shape, dt))
        wnT = sb("wnT", [D, D])
        weT = sb("weT", [D, ED])
        att = sb("att", [D, 3])
        wide = sb("att_wide", [D, 3, P])
        u = sb("through", [P, 2, D])
        prod = sb("prod", [P, BLOCKS * D])
        tab = sb("table", [P, BLOCKS, D + 2])
        zd = sb("dst_score", [P, BLOCKS])
        zdT = sb("dst_score_rows", [BLOCKS, P])
        s_in, s_v, s_p, s_t, s_c, s_out = (m.sem("l1b_" + n) for n in
                                           ("in", "vec", "product", "turned", "copied", "out"))
        at = {}
        block = ctx.enter_context(nc.Block())

        @block.vector
        def _(v):
            link = Chain(v, s_v)
            v.wait_ge(s_in, 16 * 7)
            for f in range(3):
                link(nc.vector.tensor_copy(wide[:, f, :], att[:, f:f + 1].to_broadcast([D, P])))
            at["wide"] = link.n
            v.wait_ge(s_p, 1)
            link(nc.vector.tensor_copy(u[:, 0, :], m.ps[0][0][:, 0:D]))
            link(nc.vector.tensor_copy(u[:, 1, :], m.ps[0][1][:, 0:D]))
            link(nc.vector.tensor_copy(m.ve[:, :], m.ps[0][2][:, 0:ED]))
            x = node_view(m.xs, D)
            for f, out in ((0, tab[:, :, D]), (1, zd[:, :])):
                link(nc.vector.tensor_tensor(node_view(prod, D), x, bc_mid(u[:, f, :], BLOCKS), ALU.mult))
                link(nc.vector.tensor_reduce(out, node_view(prod, D), AX.X, ALU.add))
            link(nc.vector.tensor_copy(tab[:, :, 0:D], x))
            link(nc.vector.memset(tab[:, :, D + 1:D + 2], 1.0))
            at["table"] = link.n
            v.wait_ge(s_t, 1)
            nc.vector.tensor_copy(zdT[:, :], m.ps[1][0][0:BLOCKS, 0:P]).then_inc(s_c, 1)

        @block.tensor
        def _(pe):
            pe.wait_ge(s_v, at["wide"])
            nc.tensor.matmul(m.ps[0][0][:, 0:D], wide[:, 0, :], wnT[:, :], start=True, stop=True)
            nc.tensor.matmul(m.ps[0][1][:, 0:D], wide[:, 1, :], wnT[:, :], start=True, stop=True)
            nc.tensor.matmul(m.ps[0][2][:, 0:ED], wide[:, 2, :], weT[:, :], start=True, stop=True).then_inc(s_p, 1)
            pe.wait_ge(s_v, at["table"])
            nc.tensor.transpose(m.ps[1][0][0:BLOCKS, 0:P], zd[:, :], m.ident[:, :]).then_inc(s_t, 1)

        @block.sync
        def _(sp):
            sp.dma_start(wnT[:, :], m.wnT).then_inc(s_in, 16)
            sp.dma_start(weT[:, :], m.weT).then_inc(s_in, 16)
            for f, a in enumerate((m.L1_gnn_att_src, m.L1_gnn_att_dst, m.L1_gnn_att_edge)):
                sp.dma_start(att[:, f:f + 1], a.rearrange("(d o) -> d o", o=1)).then_inc(s_in, 16)
            sp.dma_start(m.wcat[0:D, :], m.L1_gnn_Wn).then_inc(s_in, 16)
            sp.dma_start(m.wcat[D + 2:L1W, :], m.L1_gnn_We).then_inc(s_in, 16)
            sp.wait_ge(s_v, at["table"])
            sp.dma_start(m.table1.rearrange("(b p) w -> p b w", p=P), tab[:, :, :]).then_inc(s_out, 16)
            sp.wait_ge(s_c, 1)
            sp.dma_start(m.d_zd.rearrange("(b p) -> b p", p=P), zdT[:, :]).then_inc(s_out, 16)
            sp.wait_ge(s_out, 32)
            sp.dma_start(m.xb[:, :], m.d_zd.partition_broadcast(P)).then_inc(s_out, 16)
            sp.wait_ge(s_out, 48)


def layer1_scores(nc, m):
    with ExitStack() as ctx:
        sb = lambda name, shape, dt=fp32: ctx.enter_context(nc.sbuf_tensor("l1" + name, shape, dt))
        g = sb("rows", [P, UNITS, UNIT, L1W])
        idx = sb("idx", [P, UNITS, UNIT], i32)
        col = sb("columns", [P, UNITS, 1, UNIT])
        junk = sb("junk", [P, 2, UNIT, P])
        zd = sb("zd", [P, 2, UNIT])
        prod = sb("prod", [P, 2, UNIT, ED])
        se = sb("se", [P, 2, UNIT])
        gathered = [m.sem(f"l1gathered{q}") for q in range(UNITS)]
        attrs = [m.sem(f"l1attrs{q}") for q in range(UNITS)]
        stored = [m.sem(f"l1stored{q}") for q in range(UNITS)]
        s_staged, s_used, s_v = (m.sem("l1" + n) for n in ("staged", "used", "vec"))
        PER = (UNIT + 4) * UNITS
        block = ctx.enter_context(nc.Block())

        @block.vector
        def _(v):
            v.sem_inc(s_used, CREDIT)
            with nc.vector.Fori(0, TRIPS) as i:
                tick = Ticks(s_v, i, PER)
                for q in range(UNITS):
                    n, u = i * UNITS + q, q % 2
                    v.wait_ge(s_staged, done(n))
                    offsets = block_offsets(nc, m, Unit(i, q), mybir.EngineType.DVE)
                    for k in range(UNIT):
                        tick(nc.vector.scalar_tensor_tensor(
                            junk[:, u, k, :], m.iota[:, :], col[:, q, 0, k:k + 1],
                            m.xb[:, bass.ds(offsets[k], P)], ALU.is_equal, ALU.mult,
                            accum_out=zd[:, u, k:k + 1]))
                    v.wait_ge(attrs[q], 16 * UNIT * i + 16 * UNIT)
                    v.wait_ge(gathered[q], 16 * UNIT * i + 16 * UNIT)
                    v.wait_ge(s_v, tick(nc.vector.tensor_tensor(
                        prod[:, u, :, :], g[:, q, :, D + 2:L1W], bc_mid(m.ve[:, :], UNIT), ALU.mult)))
                    v.wait_ge(s_v, tick(nc.vector.tensor_reduce(se[:, u, :], prod[:, u, :, :], AX.X, ALU.add)))
                    v.wait_ge(s_v, tick(nc.vector.tensor_tensor(se[:, u, :], se[:, u, :], g[:, q, :, D], ALU.add)))
                    v.wait_ge(s_v, tick(nc.vector.tensor_tensor(se[:, u, :], se[:, u, :], zd[:, u, :], ALU.add)))
                    v.wait_ge(stored[q], 16 * i + 16)
                    nc.vector.scalar_tensor_tensor(m.scoreS[:, bass.ds(n * UNIT, UNIT)], se[:, u, :], 0.2,
                                                   se[:, u, :], ALU.mult, ALU.max).then_inc(s_used, 1)
                assert tick.n == PER

        @block.scalar
        def _(act):
            stage_first(nc, m, act, idx, col, (m.dstS,), s_used, s_staged)
            with nc.scalar.Fori(0, TRIPS) as i:
                for q in range(UNITS):
                    n = i * UNITS + q
                    stage_unit(nc, m, act, Unit(i, q + LEAD), idx, col, (m.dstS,), s_used, s_staged)
                    act.wait_ge(gathered[q], 16 * UNIT * i + 16 * UNIT)
                    act.wait_ge(attrs[q], 16 * UNIT * i + 16 * UNIT)
                    act.dma_start(m.d_rows[bass.ds(n * P, P), :],
                                  g[:, q, :, :].rearrange("p k w -> p (k w)")).then_inc(stored[q], 16)

        @block.gpsimd
        def _(pool):
            gather_rows(nc, m, pool, idx, g, D + 2, m.table1, s_staged, gathered)

        @block.sync
        def _(sp):
            load_attributes(nc, m, sp, m.ea16, lambda q, k: g[:, q, k, D + 2:L1W], UNITS, s_used, attrs)


def load_attributes(nc, m, sp, source, place, slots, s_used, came, load_more=None):
    with nc.sync.Fori(0, TRIPS) as i:
        for q in range(UNITS):
            n = i * UNITS + q
            if load_more:
                load_more(q, n)
            _, firsts = nc.values_load_multi_w_load_instructions(
                m.tile_row[0:1, bass.ds(n * UNIT, UNIT)], engines=(mybir.EngineType.SP,), min_val=0,
                max_val=(STEPS - 1) * P,
                skip_runtime_bounds_check_because="it is P times a count of begun tiles, less one")
            sp.wait_ge(s_used, done(n, slots))
            for k in range(UNIT):
                sp.dma_start(place(q, k), source[bass.ds(firsts[k], P), :]).then_inc(came[q % slots], 16)


def layer1_nodes_after(nc, m):
    with ExitStack() as ctx:
        y = ctx.enter_context(nc.sbuf_tensor("l1y", [P, BLOCKS * D], fp32))
        inv = ctx.enter_context(nc.sbuf_tensor("l1inv", [P, BLOCKS], fp32))
        s_v = m.sem("l1n_vec")
        s_v2 = m.sem("l1n_vec2")
        acc = node_view(m.acc)
        with nc.Block() as block:
            @block.vector
            def _(v):
                link = Chain(v, s_v)
                link(nc.vector.tensor_scalar(inv[:, :], acc[:, :, D + 1], 1e-8, None, ALU.add))
                link(nc.vector.reciprocal(inv[:, :], inv[:, :]))
                nc.vector.tensor_tensor(acc[:, :, 0:L1W], acc[:, :, 0:L1W], bc_last(inv[:, :], L1W), ALU.mult)
        project(nc, m, "l1p_", L1W, m.wcat, y)
        with nc.Block() as block:
            @block.vector
            def _(v):
                link = Chain(v, s_v2)
                for _ in range(2):
                    link(nc.vector.tensor_tensor(y[:, :], y[:, :], m.xs[:, :], ALU.add))
        layer_norm(nc, m, "l1ln_", y)


def layer2(nc, m):
    width = D + 1
    with ExitStack() as ctx:
        y = ctx.enter_context(nc.sbuf_tensor("l2y", [P, BLOCKS, width], fp32))
        total = ctx.enter_context(nc.sbuf_tensor("l2total", [P, BLOCKS * D], fp32))
        inv = ctx.enter_context(nc.sbuf_tensor("l2inv", [P, BLOCKS], fp32))
        with nc.Block() as block:
            @block.vector
            def _(v):
                nc.vector.memset(y[:, :, D:width], 1.0)
                nc.vector.tensor_copy(y[:, :, 0:D], node_view(m.xs, D))
        for r in range(ROUNDS):
            store_table(nc, m, f"l2_{r}", y, m.table2[r])
            weighted_sum(nc, m, f"l2_{r}", m.weightS, width, table=m.table2[r])
            m.sem.clear()
            s_v = m.sem(f"l2n_vec{r}")
            acc = node_view(m.acc)
            with nc.Block() as block:
                @block.vector
                def _(v):
                    link = Chain(v, s_v)
                    link(nc.vector.tensor_scalar(inv[:, :], acc[:, :, D], 1e-16, None, ALU.add))
                    link(nc.vector.reciprocal(inv[:, :], inv[:, :]))
                    link(nc.vector.tensor_tensor(y[:, :, 0:D], acc[:, :, 0:D], bc_last(inv[:, :], D), ALU.mult))
                    if r == ROUNDS - 1:
                        nc.vector.tensor_tensor(node_view(total, D), y[:, :, 0:D], node_view(m.xs, D), ALU.add)
        layer_norm(nc, m, "l2ln_", total)


def layer3_nodes_before(nc, m):
    with ExitStack() as ctx:
        sb = lambda name, shape, dt=fp32: ctx.enter_context(nc.sbuf_tensor("l3b" + name, shape, dt))
        w1 = sb("node1", [D, H])
        b1 = sb("b_node1", [H, 1])
        w2 = sb("node2", [H, H])
        e1 = sb("edge1", [D, H])
        e1pad = sb("edge1_padded", [P, H])
        ueT = sb("ueT_padded", [D, P])
        xT = sb("xT", [D, GROUP * P])
        r = sb("relu", [H, GROUP * P])
        part = sb("group", [P, GROUP, P])
        out = sb("rows", [P, GROUP, D + H])
        s_in, s_v, s_w, s_p, s_g, s_t, s_tc, s_h, s_r, s_m, s_o = (
            m.sem("l3b_" + n) for n in
            ("in", "vec", "weights", "product", "group", "turned", "turned_copied", "hidden", "relu",
             "rows_ready", "rows_copied"))
        s_st, s_free = m.sem("l3b_stored"), m.sem("l3b_out_free")
        halves = ((0, 4), (4, GROUP))
        block = ctx.enter_context(nc.Block())

        @block.sync
        def _(sp):
            sp.dma_start(w1[:, :], m.L3_gnn_W_node1).then_inc(s_in, 16)
            sp.dma_start(b1[:, :], m.L3_gnn_b_node1.rearrange("(d o) -> d o", o=1)).then_inc(s_in, 16)
            sp.dma_start(w2[:, :], m.L3_gnn_W_node2).then_inc(s_in, 16)
            sp.dma_start(e1[:, :], m.L3_gnn_W_edge1).then_inc(s_in, 16)
            sp.dma_start(m.be1[:, :], m.L3_gnn_b_edge1.rearrange("(d o) -> d o", o=1)).then_inc(s_in, 16)
            sp.dma_start(m.we2[:, :], m.L3_gnn_W_edge2).then_inc(s_in, 16)
            sp.dma_start(m.wcomb[:, :], m.L3_gnn_W_comb).then_inc(s_in, 16)
            sp.wait_ge(s_w, 2)
            sp.dma_start(e1pad[0:D, :], m.L3_gnn_W_edge1).then_inc(s_in, 16)
            sp.dma_start(ueT[:, D:P], m.ueT).then_inc(s_in, 16)
            sp.sem_inc(s_free, CREDIT)
            with nc.sync.Fori(0, BLOCKS // GROUP) as i:
                sp.wait_ge(s_o, done(i))
                sp.dma_start(m.table3[bass.ds(i * GROUP * P, GROUP * P), :].rearrange("(b p) w -> p b w", p=P),
                             out[:, :, :]).then_inc(s_st, 16)
                sp.wait_ge(s_st, 16 * i + 16)
                sp.sem_inc(s_free, 1)

        @block.vector
        def _(v):
            nc.vector.memset(e1pad[:, :], 0.0).then_inc(s_w, 1)
            nc.vector.memset(ueT[:, :], 0.0).then_inc(s_w, 1)
            nc.vector.memset(part[:, :, :], 0.0).then_inc(s_w, 1)
            nc.vector.tensor_copy(node_view(m.xb)[:, :, 0:D], node_view(m.xs, D))
            v.wait_ge(s_in, 16 * 9)
            v.wait_ge(s_p, 1)
            nc.vector.tensor_scalar(m.wmix[:, :], m.ps[1][3][:, 0:H], 0.2, None, ALU.mult).then_inc(s_v, 1)
            v.wait_ge(s_v, 1)
            nc.vector.scalar_tensor_tensor(m.wmix[:, :], e1pad[:, :], 0.8, m.wmix[:, :], ALU.mult, ALU.add)
            v.sem_inc(s_tc, CREDIT)
            v.sem_inc(s_o, CREDIT)
            with nc.vector.Fori(0, BLOCKS // GROUP) as i:
                v.wait_ge(s_t, done(i))
                nc.vector.tensor_copy(xT[:, 0:4 * P], m.ps[0][0][0:D, :])
                nc.vector.tensor_copy(xT[:, 4 * P:GROUP * P], m.ps[0][1][0:D, 0:3 * P]).then_inc(s_tc, 1)
                v.wait_ge(s_m, done(i))
                v.wait_ge(s_free, done(i, 1))
                v.wait_ge(s_g, done(i))
                nc.vector.tensor_copy(out[:, :, 0:D], part[:, :, 0:D])
                nc.vector.tensor_copy(out[:, 0:4, D:D + H], m.ps[1][0][:, :].rearrange("p (b d) -> p b d", d=H))
                nc.vector.tensor_copy(out[:, 4:GROUP, D:D + H],
                                      m.ps[1][1][:, 0:3 * P].rearrange("p (b d) -> p b d", d=H)).then_inc(s_o, 1)

        @block.tensor
        def _(pe):
            for s in (s_t, s_h, s_m):
                pe.sem_inc(s, CREDIT)
            pe.wait_ge(s_in, 16 * 9)
            nc.tensor.matmul(m.ps[1][3][:, 0:H], ueT[:, :], e1[:, :], start=True, stop=True).then_inc(s_p, 1)
            with nc.tensor.Fori(0, BLOCKS // GROUP) as i:
                pe.wait_ge(s_g, done(i))
                pe.wait_ge(s_tc, done(i, 1))
                for k in range(GROUP):
                    last = nc.tensor.transpose(m.ps[0][k // 4][:, k % 4 * P:(k % 4 + 1) * P],
                                               part[:, k, :], m.ident[:, :])
                last.then_inc(s_t, 1)
                pe.wait_ge(s_tc, done(i))
                pe.wait_ge(s_r, done(i, 1))
                for c, (lo, hi) in enumerate(halves):
                    last = nc.tensor.matmul(m.ps[0][2 + c][:, 0:(hi - lo) * P], w1[:, :],
                                            xT[:, lo * P:hi * P], start=True, stop=True)
                last.then_inc(s_h, 1)
                pe.wait_ge(s_r, done(i))
                pe.wait_ge(s_o, done(i, 1))
                for k in range(GROUP):
                    last = nc.tensor.matmul(m.ps[1][k // 4][:, k % 4 * H:(k % 4 + 1) * H],
                                            r[:, k * P:(k + 1) * P], w2[:, :], start=True, stop=True)
                last.then_inc(s_m, 1)

        @block.scalar
        def _(act):
            act.sem_inc(s_g, CREDIT)
            act.sem_inc(s_r, CREDIT)
            act.wait_ge(s_in, 16 * 9)
            act.wait_ge(s_w, 3)
            with nc.scalar.Fori(0, BLOCKS // GROUP) as i:
                act.wait_ge(s_o, done(i, 1))
                nc.scalar.copy(part[:, :, 0:D], m.xs[:, bass.ds(i * GROUP * D, GROUP * D)].rearrange(
                    "p (b d) -> p b d", d=D)).then_inc(s_g, 1)
                act.wait_ge(s_h, done(i))
                for c, (lo, hi) in enumerate(halves):
                    last = nc.scalar.activation(r[:, lo * P:hi * P], m.ps[0][2 + c][:, 0:(hi - lo) * P],
                                                ACT.Relu, bias=b1[:, 0:1])
                last.then_inc(s_r, 1)


def layer3_edges(nc, m):
    with ExitStack() as ctx:
        sb = lambda name, shape, dt=fp32: ctx.enter_context(nc.sbuf_tensor("l3" + name, shape, dt))
        W3 = D + H
        SLOTS = 4
        g = sb("rows", [P, UNITS, UNIT, W3])
        idx = sb("idx", [P, UNITS, UNIT], i32)
        col = sb("columns", [P, UNITS, 1, UNIT])
        pre = sb("pre", [P, SLOTS, UNIT, P])
        oh = sb("onehot", [P, UNITS, UNIT, P])
        dstb = sb("dst_all", [P, SLOTS, UNIT * P], bf16)
        ohT = sb("onehotT", [P, 2, UNIT * P])
        preT = sb("preT", [P, 2, UNIT * P])
        r = sb("relu", [P, 2, UNIT * P])
        both = sb("both", [P, 2, UNIT, H])
        bothT = sb("bothT", [P, 2, UNIT * P])
        val = sb("values", [P, 2, UNIT * D])
        gathered = [m.sem(f"l3gathered{q}") for q in range(UNITS)]
        dsts = [m.sem(f"l3dsts{q}") for q in range(SLOTS)]
        attrs = [m.sem(f"l3attrs{q}") for q in range(SLOTS)]
        (s_staged, s_oh, s_ohT, s_hd, s_pre, s_pt, s_ptc, s_mix, s_r, s_m2, s_both, s_bt, s_btc, s_comb,
         s_val, s_sum, s_add) = (m.sem("l3" + n) for n in
                                 ("staged", "onehot_ready", "onehotT_ready", "dst_rows",
                                  "pre_ready", "pre_turned", "preT_copied", "mixed", "relu_ready", "m2_ready",
                                  "both_ready", "both_turned", "bothT_copied", "combined", "values_ready",
                                  "summed", "added"))
        block = ctx.enter_context(nc.Block())

        @block.vector
        def _(v):
            def products(unit):
                v.wait_ge(s_m2, done(unit.n))
                v.wait_ge(s_bt, done(unit.n, 2))
                nc.vector.tensor_tensor(both[:, unit.parity, :, :], g[:, unit.slot, :, D:W3],
                                        m.ps[unit.parity][0][:, :].rearrange("p (k d) -> p k d", d=H),
                                        ALU.mult).then_inc(s_both, 1)

            def onehot(unit, k):
                return nc.vector.tensor_scalar(oh[:, unit.slot, k, :], m.iota[:, :],
                                               col[:, unit.slot, 0, k:k + 1], None, ALU.is_equal)

            def onehotT(unit):
                v.wait_ge(dsts[unit.slot % SLOTS], 16 * (unit.turns * 2 - (1 if unit.slot < SLOTS else 0)))
                v.wait_ge(s_hd, done(unit.n, 2))
                nc.vector.tensor_scalar(ohT[:, unit.parity, :], dstb[:, unit.slot % SLOTS, :],
                                        m.step_col[:, 0:1], None, ALU.is_equal).then_inc(s_ohT, 1)

            def node_products(unit):
                v.wait_ge(s_hd, done(unit.n))
                v.wait_ge(s_pt, done(unit.n, SLOTS))
                v.wait_ge(gathered[unit.slot], 16 * UNIT * unit.turns)
                nc.vector.tensor_tensor(
                    pre[:, unit.slot % SLOTS, :, D:P], g[:, unit.slot, :, 0:D],
                    m.ps[unit.parity][1][:, 0:UNIT * D].rearrange("p (k d) -> p k d", d=D),
                    ALU.mult).then_inc(s_pre, 1)

            def copy_pre(unit):
                v.wait_ge(s_pt, done(unit.n))
                v.wait_ge(s_mix, done(unit.n, 2))
                nc.vector.tensor_copy(preT[:, unit.parity, :], m.ps[unit.parity][2][:, :]).then_inc(s_ptc, 1)

            def trip_body(trip):
                for j in range(UNITS):
                    unit = at_stage(trip, j, 4)
                    if unit:
                        products(unit)
                    unit = at_stage(trip, j, 1)
                    if unit:
                        node_products(unit)
                    fresh, late = at_stage(trip, j, 0), at_stage(trip, j, 7)
                    if fresh:
                        v.wait_ge(s_staged, done(fresh.n))
                        v.wait_ge(s_sum, done(fresh.n, UNITS))
                    build_and_add(nc, m, v, fresh, late, onehot, D, s_sum, s_add, s_oh)
                    unit = at_stage(trip, j, 1)
                    if unit:
                        copy_pre(unit)
                    if fresh:
                        onehotT(fresh)

            for s in (s_oh, s_ohT, s_pre, s_ptc, s_both):
                v.sem_inc(s, CREDIT)
            nc.vector.memset(m.acc[:, :], 0.0).then_inc(s_add, 1)
            run_trips(nc.vector, trip_body)

        @block.tensor
        def _(pe):
            def dst_rows(unit):
                offsets = block_offsets(nc, m, unit, mybir.EngineType.PE)
                pe.wait_ge(s_ohT, done(unit.n))
                pe.wait_ge(s_val, done(unit.n, 6))
                for k in range(UNIT):
                    last = nc.tensor.matmul(m.ps[unit.parity][1][:, k * D:(k + 1) * D],
                                            ohT[:, unit.parity, k * P:(k + 1) * P],
                                            m.xb[:, bass.ds(offsets[k], D)], start=True, stop=True)
                last.then_inc(s_hd, 1)

            def turn_pre(unit):
                pe.wait_ge(s_pre, done(unit.n))
                pe.wait_ge(attrs[unit.slot % SLOTS],
                           16 * UNIT * (unit.turns * 2 - (1 if unit.slot < SLOTS else 0)))
                pe.wait_ge(s_btc, done(unit.n, 4))
                for k in range(UNIT):
                    last = nc.tensor.transpose(m.ps[unit.parity][2][:, k * P:(k + 1) * P],
                                               pre[:, unit.slot % SLOTS, k, :], m.ident[:, :])
                last.then_inc(s_pt, 1)

            def mix(unit):
                pe.wait_ge(s_ptc, done(unit.n))
                wait_added(pe, unit, 6, s_add)
                nc.tensor.matmul(m.ps[unit.parity][3][:, :], m.wmix[:, :], preT[:, unit.parity, :],
                                 start=True, stop=True).then_inc(s_mix, 1)

            def second_edge_product(unit):
                pe.wait_ge(s_r, done(unit.n))
                pe.wait_ge(s_both, done(unit.n, 2))
                for k in range(UNIT):
                    last = nc.tensor.matmul(m.ps[unit.parity][0][:, k * H:(k + 1) * H],
                                            r[:, unit.parity, k * P:(k + 1) * P], m.we2[:, :],
                                            start=True, stop=True)
                last.then_inc(s_m2, 1)

            def turn_products(unit):
                pe.wait_ge(s_both, done(unit.n))
                wait_bank(pe, unit, 2, s_ptc, s_btc)
                for k in range(UNIT):
                    last = nc.tensor.transpose(m.ps[unit.parity][2][:, k * P:(k + 1) * P],
                                               both[:, unit.parity, k, :], m.ident[:, :])
                last.then_inc(s_bt, 1)

            def combine(unit):
                pe.wait_ge(s_btc, done(unit.n))
                wait_bank(pe, unit, 4, s_pre, s_val)
                for k in range(UNIT):
                    last = nc.tensor.matmul(m.ps[unit.parity][1][:, k * D:(k + 1) * D],
                                            bothT[:, unit.parity, k * P:(k + 1) * P], m.wcomb[:, :],
                                            start=True, stop=True)
                last.then_inc(s_comb, 1)

            def sums(unit):
                pe.wait_ge(s_val, done(unit.n))
                wait_added(pe, unit, 2, s_add)
                if not isinstance(unit.n, int) or unit.n + 4 < ALL_UNITS:
                    pe.wait_ge(s_r, done(unit.n + 4))
                for k in range(UNIT):
                    last = nc.tensor.matmul(m.ps[unit.parity][3][:, k * D:(k + 1) * D], oh[:, unit.slot, k, :],
                                            val[:, unit.parity, k * D:(k + 1) * D], start=True, stop=True)
                last.then_inc(s_sum, 1)

            def trip_body(trip):
                for j in range(UNITS):
                    for lag, stage in ((6, combine), (1, dst_rows), (7, sums), (4, turn_products),
                                       (1, turn_pre), (2, mix), (3, second_edge_product)):
                        unit = at_stage(trip, j, lag)
                        if unit:
                            stage(unit)

            for s in (s_hd, s_pt, s_mix, s_m2, s_bt, s_comb, s_sum):
                pe.sem_inc(s, CREDIT)
            run_trips(nc.tensor, trip_body)

        @block.scalar
        def _(act):
            def relu(unit):
                act.wait_ge(s_mix, done(unit.n))
                act.wait_ge(s_m2, done(unit.n, 2))
                nc.scalar.activation(r[:, unit.parity, :], m.ps[unit.parity][3][:, :], ACT.Relu,
                                     bias=m.be1[:, 0:1]).then_inc(s_r, 1)

            def copy_products(unit):
                act.wait_ge(s_bt, done(unit.n))
                act.wait_ge(s_comb, done(unit.n, 2))
                nc.scalar.copy(bothT[:, unit.parity, :], m.ps[unit.parity][2][:, :]).then_inc(s_btc, 1)

            def tanh(unit):
                act.wait_ge(s_comb, done(unit.n))
                act.wait_ge(s_sum, done(unit.n, 2))
                nc.scalar.activation(val[:, unit.parity, :], m.ps[unit.parity][1][:, 0:UNIT * D],
                                     ACT.Tanh).then_inc(s_val, 1)

            def trip_body(trip):
                for j in range(UNITS):
                    for lag, stage in ((2, relu),
                                       (-LEAD, lambda unit: stage_unit(nc, m, act, unit, idx, col, (m.dstS,),
                                                                       s_both, s_staged)),
                                       (6, tanh), (4, copy_products)):
                        unit = at_stage(trip, j, lag)
                        if unit:
                            stage(unit)

            for s in (s_r, s_btc, s_val):
                act.sem_inc(s, CREDIT)
            stage_first(nc, m, act, idx, col, (m.dstS,), s_both, s_staged)
            run_trips(nc.scalar, trip_body)

        @block.gpsimd
        def _(pool):
            gather_rows(nc, m, pool, idx, g, W3, m.table3, s_staged, gathered)

        @block.sync
        def _(sp):
            def load_dst(q, n):
                sp.wait_ge(s_ohT, done(n, SLOTS))
                sp.dma_start(dstb[:, q % SLOTS, :], m.d_dst[:, bass.ds(n * UNIT * P, UNIT * P)].to_broadcast(
                    [P, UNIT * P])).then_inc(dsts[q % SLOTS], 16)

            load_attributes(nc, m, sp, m.ea64, lambda q, k: pre[:, q % SLOTS, k, 0:D], SLOTS, s_pt, attrs,
                            load_dst)


def layer3_nodes_after(nc, m):
    with ExitStack() as ctx:
        y = ctx.enter_context(nc.sbuf_tensor("l3y", [P, BLOCKS * D], fp32))
        s_v, s_out = m.sem("l3n_vec"), m.sem("l3n_out")
        with nc.Block() as block:
            @block.vector
            def _(v):
                link = Chain(v, s_v)
                link(nc.vector.tensor_tensor(node_view(y, D), node_view(m.acc)[:, :, 0:D], node_view(m.xs, D),
                                             ALU.add))
                link(nc.vector.tensor_tensor(y[:, :], y[:, :], m.xs[:, :], ALU.add))
        layer_norm(nc, m, "l3ln_", y)
        with nc.Block() as block:
            @block.sync
            def _(sp):
                full = N // P
                sp.dma_start(m.out[0:full * P].rearrange("(b p) d -> p b d", p=P),
                             node_view(m.xs, D)[:, 0:full, :]).then_inc(s_out, 16)
                sp.dma_start(m.out[full * P:N], m.xs[0:N - full * P, full * D:(full + 1) * D]).then_inc(s_out, 16)
                sp.wait_ge(s_out, 32)


def build(nc, a):
    ctx = ExitStack()
    with ctx:
        m = Program()
        m.L0_gnn_gamma_gathered_b = a["L0_gnn_gamma_gathered_b"]
        m.L0_gnn_gamma_gathered_w = a["L0_gnn_gamma_gathered_w"]
        m.L0_gnn_gamma_self_w = a["L0_gnn_gamma_self_w"]
        m.L0_gnn_mlp_b1 = a["L0_gnn_mlp_b1"]
        m.L0_gnn_mlp_b2 = a["L0_gnn_mlp_b2"]
        m.L0_gnn_mlp_w1 = a["L0_gnn_mlp_w1"]
        m.L0_gnn_mlp_w2 = a["L0_gnn_mlp_w2"]
        m.L0_gnn_pd_a = a["L0_gnn_pd_a"]
        m.L0_gnn_pd_b = a["L0_gnn_pd_b"]
        m.L1_gnn_We = a["L1_gnn_We"]
        m.L1_gnn_Wn = a["L1_gnn_Wn"]
        m.L1_gnn_att_dst = a["L1_gnn_att_dst"]
        m.L1_gnn_att_edge = a["L1_gnn_att_edge"]
        m.L1_gnn_att_src = a["L1_gnn_att_src"]
        m.L3_gnn_W_comb = a["L3_gnn_W_comb"]
        m.L3_gnn_W_edge1 = a["L3_gnn_W_edge1"]
        m.L3_gnn_W_edge2 = a["L3_gnn_W_edge2"]
        m.L3_gnn_W_node1 = a["L3_gnn_W_node1"]
        m.L3_gnn_W_node2 = a["L3_gnn_W_node2"]
        m.L3_gnn_b_edge1 = a["L3_gnn_b_edge1"]
        m.L3_gnn_b_node1 = a["L3_gnn_b_node1"]
        m.c_ident = a["c_ident"]
        m.c_iota = a["c_iota"]
        m.c_step = a["c_step"]
        m.dst_flat = a["dst_flat"]
        m.ea16 = a["ea16"]
        m.ea64 = a["ea64"]
        m.ew = a["ew"]
        m.ew2 = a["ew2"]
        m.out = a["out"]
        m.src = a["src"]
        m.ueT = a["ueT"]
        m.weT = a["weT"]
        m.wnT = a["wnT"]
        m.x = a["x"]
        m.sem = Semaphores(nc)
        sb = lambda name, shape, dt: ctx.enter_context(nc.sbuf_tensor(name, shape, dt))
        dr = lambda name, shape: nc.dram_tensor(name, shape, fp32).ap()
        m.ps = [[ctx.enter_context(nc.psum_tensor(f"ps{u}{x}", [P, 512], fp32)) for x in range(4)]
                for u in range(2)]
        m.ident = sb("ident", [P, P], fp32)
        m.iota = sb("iota", [P, P], fp32)
        m.step_col = sb("step_col", [P, CHUNKS], fp32)
        m.dstS = sb("dst_steps", [P, STEPS + LEAD * UNIT], fp32)
        m.srcS = sb("src_steps", [P, STEPS + LEAD * UNIT], fp32)
        m.ewS = sb("ew_steps", [P, STEPS + LEAD * UNIT], fp32)
        m.binS = sb("bin_steps", [P, STEPS + LEAD * UNIT], fp32)
        m.ew2S = sb("ew2_steps", [P, STEPS + LEAD * UNIT], fp32)
        m.tile_row = sb("tile_row", [1, STEPS], i32)
        m.off_row = sb("offset_row", [1, STEPS], i32)
        m.d_extra = dr("d_extra", (STEPS,))
        m.d_pos = dr("d_pos", (STEPS,))
        m.d_q = dr("d_q", (STEPS, QW))
        m.d_tb = dr("d_tb", (2, STEPS))
        m.d_start, m.d_end, m.d_ewm, m.d_mine = (dr(name, (STEPS * P,)) for name in
                                                 ("d_start", "d_end", "d_ewm", "d_mine"))
        m.d_dst = nc.dram_tensor("d_dst", (1, STEPS * P), bf16).ap()
        m.d_ew = dr("d_ew", (1, STEPS * P))
        m.d_score = dr("d_score", (STEPS * P,))
        m.d_weight = dr("d_weight", (STEPS * P,))
        m.d_tail = dr("d_tail", (2, 2, P))
        m.d_carry = dr("d_carry", (2, P))
        m.weightS = sb("weight_steps", [P, STEPS + LEAD * UNIT], fp32)
        m.scoreS = sb("score_steps", [P, STEPS], fp32)
        m.ve = sb("edge_att", [P, ED], fp32)
        m.wcat = sb("wcat", [L1W, D], fp32)
        m.be1 = sb("b_edge1", [H, 1], fp32)
        m.we2 = sb("w_edge2", [H, H], fp32)
        m.wcomb = sb("w_comb", [H, D], fp32)
        m.wmix = sb("w_mix", [P, H], fp32)
        m.table1 = dr("table1", (NPAD, D + 2))
        m.table2 = [dr(f"table2_{r}", (NPAD, D + 1)) for r in range(ROUNDS)]
        m.table3 = dr("table3", (NPAD, D + H))
        m.d_zd = dr("d_zd", (NPAD,))
        m.d_rows = dr("d_rows", (STEPS // UNIT * P, UNIT * L1W))
        m.w1 = sb("w1", [D, 1], fp32)
        m.b1 = sb("b1", [D, 1], fp32)
        m.w2b = sb("w2b", [D + 1, BINS], fp32)
        m.gw = sb("gw", [P, D], fp32)
        m.gb = sb("gb", [P, D], fp32)
        m.a, m.b, m.low, m.na, m.tiny = (sb("pd_" + name, [P, 1], fp32) for name in
                                        ("a", "b", "low", "na", "tiny"))
        load_edges(nc, m)
        place_steps(nc, m)
        m.acc = sb("acc", [P, BLOCKS * P], fp32)
        m.xb = sb("node_rows", [P, BLOCKS * P], fp32)
        m.xs = sb("node_x", [P, BLOCKS * D], fp32)
        layer0_nodes_before(nc, m)
        layer0_edges(nc, m)
        layer0_nodes_after(nc, m)
        m.sem.clear()
        layer1_nodes_before(nc, m)
        layer1_scores(nc, m)
        m.sem.clear()
        edge_softmax(nc, m, "w1_", m.weightS, score=m.scoreS, floor=-1e9)
        weighted_sum(nc, m, "l1_", m.weightS, L1W, stored=m.d_rows)
        layer1_nodes_after(nc, m)
        m.sem.clear()
        edge_softmax(nc, m, "w2_", m.weightS)
        layer2(nc, m)
        m.sem.clear()
        layer3_nodes_before(nc, m)
        layer3_edges(nc, m)
        layer3_nodes_after(nc, m)


def kernel(**inputs):
    import concourse.bacc as _bacc
    from concourse.bass_utils import run_bass_kernel_spmd as _run

    nc = _bacc.Bacc("TRN2", target_bir_lowering=False, num_devices=1)
    x = {k: np.asarray(v) for k, v in inputs.items()}
    rows = STEPS * P

    def padded(v, fill):
        out = np.full((rows,) + v.shape[1:], fill, v.dtype)
        out[:E] = v
        return out

    dst = np.full(rows + 2, PAD_NODE, np.int32)
    dst[0], dst[-1] = -1, NPAD
    dst[1:E + 1] = x["dst"]
    nodes = np.zeros((NPAD, D), np.float32)
    nodes[:N] = x["x"]
    arrays = {
        "x": nodes,
        "dst_flat": dst,
        "src": padded(x["src"], 0).reshape(STEPS, P),
        "ew": padded(x["edge_weight"], 0).reshape(STEPS, P),
        "ew2": padded(x["edge_weight_n2"], 0).reshape(STEPS, P),
        "ea16": padded(x["edge_attr_16"], 0),
        "ea64": padded(x["edge_attr_64"], 0),
        "c_ident": np.eye(P, dtype=np.float32),
        "c_iota": np.tile(np.arange(P, dtype=np.float32), (P, 1)),
        "c_step": np.ascontiguousarray(np.arange(STEPS, dtype=np.float32).reshape(CHUNKS, P).T),
        "wnT": np.ascontiguousarray(x["L1_gnn_Wn"].T),
        "ueT": np.ascontiguousarray(x["L3_gnn_W_ue"].T),
        "weT": np.ascontiguousarray(x["L1_gnn_We"].T),
    }
    for k, v in x.items():
        if k.startswith("L"):
            arrays[k] = np.ascontiguousarray(v)
    a = {}
    for k, v in arrays.items():
        a[k] = nc.dram_tensor(k, v.shape, mybir.dt.from_np(v.dtype), kind="ExternalInput").ap()
    a["out"] = nc.dram_tensor("out", (N, D), fp32, kind="ExternalOutput").ap()
    build(nc, a)
    r = _run(nc, [arrays], core_ids=[0])
    return r.results[0]["out"]
```
